# Optimizing a Trainium2 kernel written in Bass

```python
import numpy as np
import jax
import jax.numpy as jnp

def _softmax(x, axis=-1):
    return jax.nn.softmax(x, axis=axis)

def _gelu(x):
    return jax.nn.gelu(x, approximate=True)

def _silu(x):
    return jax.nn.silu(x)

def _sigmoid(x):
    return jax.nn.sigmoid(x)

def _layernorm(x, axis=-1, eps=1e-05):
    m = jnp.mean(x, axis=axis, keepdims=True)
    v = jnp.var(x, axis=axis, keepdims=True)
    return (x - m) / jnp.sqrt(v + eps)

def _scatter_add(tgt, idx, src, axis=0):
    return tgt.at[idx].add(src)

def _segment_sum(src, seg, n):
    return jax.ops.segment_sum(src, seg, n)
kernel_name = 'mk_gnn_ffn_d1_gnn_r8_c108a9'

def setup_inputs(seed: int=0):
    np.random.seed(seed)
    _w = jnp.asarray

    def _rec_inputs():
        import jax
        import jax.numpy as jnp
        _gk = jax.random.key(seed)
        x = -0.0003713 + 1 * jax.random.normal(jax.random.fold_in(_gk, 1), (6250, 256), jnp.float32)
        _s = jax.random.randint(jax.random.fold_in(_gk, 2), (100000,), 0, 6250, jnp.int32)
        _d = jax.random.randint(jax.random.fold_in(_gk, 3), (100000,), 0, 6250, jnp.int32)
        _loop = jnp.arange(6250, dtype=jnp.int32)
        src = jnp.concatenate([_s, _d, _loop])
        dst = jnp.concatenate([_d, _s, _loop])
        _o = jnp.argsort(dst, stable=True)
        src = src[_o]
        dst = dst[_o]
        return (x, src, dst)
    x, src, dst = _rec_inputs()

    def _L0_gnn_setup():
        import jax, jax.numpy as jnp
        import numpy as np
        ALPHA = 0.2
        LN_EPS = 1e-05

        def _gat_layer(x, src, dst, W, b, a, g, beta, N, concat):
            h = x @ W.T + b
            d = W.shape[0]
            s_src = h @ a[:d]
            s_dst = h @ a[d:]
            score = s_src[src] + s_dst[dst]
            e = jnp.exp(-jax.nn.leaky_relu(score, ALPHA))
            h_prime = jax.ops.segment_sum(e[:, None] * h[dst], src, num_segments=N)
            mu = jnp.mean(h_prime, axis=-1, keepdims=True)
            var = jnp.var(h_prime, axis=-1, keepdims=True)
            h_prime = (h_prime - mu) * jax.lax.rsqrt(var + LN_EPS) * g + beta
            return jax.nn.elu(h_prime) if concat else h_prime
        key = jax.random.key(seed)
        ks = jax.random.split(key, 13)
        N, E, F, D, H = (6250, 100000, 256, 64, 8)
        S = 0.02
        inp = {'embeds': jax.random.normal(ks[0], (N, F), dtype=jnp.float32), 'W_heads': jax.random.normal(ks[1], (H, D, F), dtype=jnp.float32) * S, 'b_heads': jax.random.normal(ks[2], (H, D), dtype=jnp.float32) * S, 'a_heads': jax.random.normal(ks[3], (H, 2 * D), dtype=jnp.float32) * S, 'g_heads': jnp.ones((H, D), dtype=jnp.float32), 'beta_heads': jnp.zeros((H, D), dtype=jnp.float32), 'W_out': jax.random.normal(ks[4], (F, D * H), dtype=jnp.float32) * S, 'b_out': jax.random.normal(ks[5], (F,), dtype=jnp.float32) * S, 'a_out': jax.random.normal(ks[6], (2 * F,), dtype=jnp.float32) * S, 'g_out': jnp.ones((F,), dtype=jnp.float32), 'beta_out': jnp.zeros((F,), dtype=jnp.float32), 'edge_index': jax.random.randint(ks[7], (2, E), 0, N, dtype=jnp.int32)}
        return inp
    _L0_gnn_all = _L0_gnn_setup()
    _L0_gnn_in = {k: v for k, v in _L0_gnn_all.items() if k in ('W_heads', 'b_heads', 'a_heads', 'g_heads', 'beta_heads', 'W_out', 'b_out', 'a_out', 'g_out', 'beta_out')}
    del _L0_gnn_all

    def _L0_ffn_setup():
        import jax, jax.numpy as jnp
        import numpy as np
        NUM_EXPERTS = 8
        TOP_K = 2
        B, S, D = (8, 1024, 256)

        def _moe(tokens, router_w, w1, b1, w2, b2):
            N = tokens.shape[0]
            E = router_w.shape[0]
            logits = tokens.astype(jnp.float32) @ router_w.astype(jnp.float32).T
            probs = jax.nn.softmax(logits, axis=-1)
            rw, re = jax.lax.top_k(probs, TOP_K)
            if TOP_K > 1:
                rw = rw / jnp.maximum(rw.sum(-1, keepdims=True), 1e-12)
            rw = rw.astype(tokens.dtype)
            combine = jnp.zeros((N, E), tokens.dtype).at[jnp.arange(N)[:, None], re].set(rw)
            out = tokens
            for e in range(E):
                h = jax.nn.gelu(tokens @ w1[e] + b1[e], approximate=False)
                y = h @ w2[e] + b2[e]
                out = out + combine[:, e:e + 1] * y
            return out
        key = jax.random.key(seed)
        ks = jax.random.split(key, 4)
        scale = 1.0 / np.sqrt(D).astype(np.float32)
        return {'input_embeddings': jax.random.normal(ks[0], (B, S, D), jnp.float32), 'router_w': jax.random.normal(ks[1], (NUM_EXPERTS, D), jnp.float32) * scale, 'w1': jax.random.normal(ks[2], (NUM_EXPERTS, D, D), jnp.float32) * scale, 'b1': jnp.zeros((NUM_EXPERTS, D), jnp.float32), 'w2': jax.random.normal(ks[3], (NUM_EXPERTS, D, D), jnp.float32) * scale, 'b2': jnp.zeros((NUM_EXPERTS, D), jnp.float32)}
    _L0_ffn_all = _L0_ffn_setup()
    _L0_ffn_in = {k: v for k, v in _L0_ffn_all.items() if k in ('router_w', 'w1', 'b1', 'w2', 'b2')}
    del _L0_ffn_all
    return {'x': x, 'src': src, 'dst': dst, 'L0_gnn_W_heads': _L0_gnn_in['W_heads'], 'L0_gnn_b_heads': _L0_gnn_in['b_heads'], 'L0_gnn_a_heads': _L0_gnn_in['a_heads'], 'L0_gnn_g_heads': _L0_gnn_in['g_heads'], 'L0_gnn_beta_heads': _L0_gnn_in['beta_heads'], 'L0_gnn_W_out': _L0_gnn_in['W_out'], 'L0_gnn_b_out': _L0_gnn_in['b_out'], 'L0_gnn_a_out': _L0_gnn_in['a_out'], 'L0_gnn_g_out': _L0_gnn_in['g_out'], 'L0_gnn_beta_out': _L0_gnn_in['beta_out'], 'L0_ffn_router_w': _L0_ffn_in['router_w'], 'L0_ffn_w1': _L0_ffn_in['w1'], 'L0_ffn_b1': _L0_ffn_in['b1'], 'L0_ffn_w2': _L0_ffn_in['w2'], 'L0_ffn_b2': _L0_ffn_in['b2']}

def reference(x, src, dst, L0_gnn_W_heads, L0_gnn_b_heads, L0_gnn_a_heads, L0_gnn_g_heads, L0_gnn_beta_heads, L0_gnn_W_out, L0_gnn_b_out, L0_gnn_a_out, L0_gnn_g_out, L0_gnn_beta_out, L0_ffn_router_w, L0_ffn_w1, L0_ffn_b1, L0_ffn_w2, L0_ffn_b2):
    import jax
    import jax.numpy as jnp

    def _L0_gnn_ref(embeds, W_heads, b_heads, a_heads, g_heads, beta_heads, W_out, b_out, a_out, g_out, beta_out, edge_index):
        import jax, jax.numpy as jnp
        import numpy as np
        ALPHA = 0.2
        LN_EPS = 1e-05

        def _gat_layer(x, src, dst, W, b, a, g, beta, N, concat):
            h = x @ W.T + b
            d = W.shape[0]
            s_src = h @ a[:d]
            s_dst = h @ a[d:]
            score = s_src[src] + s_dst[dst]
            e = jnp.exp(-jax.nn.leaky_relu(score, ALPHA))
            h_prime = jax.ops.segment_sum(e[:, None] * h[dst], src, num_segments=N)
            mu = jnp.mean(h_prime, axis=-1, keepdims=True)
            var = jnp.var(h_prime, axis=-1, keepdims=True)
            h_prime = (h_prime - mu) * jax.lax.rsqrt(var + LN_EPS) * g + beta
            return jax.nn.elu(h_prime) if concat else h_prime
        N = embeds.shape[0]
        src, dst = (edge_index[0], edge_index[1])
        H = W_heads.shape[0]
        heads = [_gat_layer(embeds, src, dst, W_heads[i], b_heads[i], a_heads[i], g_heads[i], beta_heads[i], N, concat=True) for i in range(H)]
        x = jnp.concatenate(heads, axis=1)
        out = _gat_layer(x, src, dst, W_out, b_out, a_out, g_out, beta_out, N, concat=False)
        return jax.nn.elu(out)

    def _L0_ffn_ref(input_embeddings, router_w, w1, b1, w2, b2):
        import jax, jax.numpy as jnp
        import numpy as np
        NUM_EXPERTS = 8
        TOP_K = 2
        B, S, D = (8, 1024, 256)

        def _moe(tokens, router_w, w1, b1, w2, b2):
            N = tokens.shape[0]
            E = router_w.shape[0]
            logits = tokens.astype(jnp.float32) @ router_w.astype(jnp.float32).T
            probs = jax.nn.softmax(logits, axis=-1)
            rw, re = jax.lax.top_k(probs, TOP_K)
            if TOP_K > 1:
                rw = rw / jnp.maximum(rw.sum(-1, keepdims=True), 1e-12)
            rw = rw.astype(tokens.dtype)
            combine = jnp.zeros((N, E), tokens.dtype).at[jnp.arange(N)[:, None], re].set(rw)
            out = tokens
            for e in range(E):
                h = jax.nn.gelu(tokens @ w1[e] + b1[e], approximate=False)
                y = h @ w2[e] + b2[e]
                out = out + combine[:, e:e + 1] * y
            return out
        b, s, d = input_embeddings.shape
        tokens = input_embeddings.reshape(b * s, d)
        return _moe(tokens, router_w, w1, b1, w2, b2).reshape(b, s, d)
    edge_index = jnp.stack([src, dst])
    x = x + _L0_gnn_ref(_layernorm(x, axis=-1), L0_gnn_W_heads, L0_gnn_b_heads, L0_gnn_a_heads, L0_gnn_g_heads, L0_gnn_beta_heads, L0_gnn_W_out, L0_gnn_b_out, L0_gnn_a_out, L0_gnn_g_out, L0_gnn_beta_out, edge_index)
    x = x + _L0_ffn_ref(_layernorm(x, axis=-1)[None], L0_ffn_router_w, L0_ffn_w1, L0_ffn_b1, L0_ffn_w2, L0_ffn_b2)[0]
    return x

_drawn_inputs = setup_inputs


def setup_inputs(seed=0):
    import zlib

    import numpy as np

    out = dict(_drawn_inputs(seed))
    spreads = {'L0_gnn_g_heads': (1.0, 0.2),
     'L0_gnn_beta_heads': (0.0, 0.1),
     'L0_gnn_g_out': (1.0, 0.2),
     'L0_gnn_beta_out': (0.0, 0.1),
     'L0_ffn_b1': (0.0, 0.381),
     'L0_ffn_b2': (0.0, 0.1)}
    factors = {}
    for name, (base, spread) in spreads.items():
        noise = np.random.default_rng([zlib.crc32(name.encode()), seed]).standard_normal(out[name].shape)
        drawn = base * np.exp(spread * noise) if base else spread * noise
        out[name] = jnp.asarray(drawn.astype(out[name].dtype))
    for name, factor in factors.items():
        out[name] = (out[name] * factor).astype(out[name].dtype)
    return out
```

```python
import concourse.bass as bass
from concourse import mybir
from contextlib import ExitStack

FP32 = mybir.dt.float32
BF16 = mybir.dt.bfloat16
FP16 = mybir.dt.float16
I32 = mybir.dt.int32
U16 = mybir.dt.uint16
U32 = mybir.dt.uint32
ALU = mybir.AluOpType
ACT = mybir.ActivationFunctionType
AX = mybir.AxisListType

P = 128
NODES = 6250
FEAT = 256
HEADS = 8
HDIM = 64
HD = HEADS * HDIM
EDGES = 206250
EXPERTS = 8
LN_EPS = 1e-5
SLOPE = 0.2

BLOCKS = -(-NODES // P)
LAST = NODES - (BLOCKS - 1) * P
CHUNK_BLOCKS = 7
CHUNKS = BLOCKS // CHUNK_BLOCKS
assert CHUNKS * CHUNK_BLOCKS == BLOCKS

EP = max(p for p in range(1, P + 1) if EDGES % p == 0)
ECOLS = EDGES // EP
PARTS = 3
PCOLS = ECOLS // PARTS
PHALF = PCOLS // 2
assert PARTS * PCOLS == ECOLS and 2 * PHALF == PCOLS
PART_TILES = -(-(EP * PCOLS // P + BLOCKS) // 2) * 2
THALF = PART_TILES // 2
GROUP = 4
RING = 6
STEPS = -(-(PARTS * PART_TILES) // GROUP) * GROUP
GROUPS = STEPS // GROUP
ROUNDS = (GROUPS - GROUP) // RING
DST_LOW = 1024
MAGIC = 1.5 * 2.0 ** 23
SUM_BANKS = 3
IDLE_BANK, SPARE_BANK = 3, 4
NOWHERE = 100000.0
NO_NODE = 1000.0

ROW1 = HD + HEADS
ROW2 = FEAT + 4


class Chain:

    def __init__(self, eng, sem, base=0):
        self.eng, self.sem, self.base, self.n = eng, sem, base, 0

    def mark(self, ins):
        ins.then_inc(self.sem, 1)
        self.n += 1

    def wait(self):
        self.eng.wait_ge(self.sem, self.base + self.n)


def hold(eng, sem, value, scratch):
    eng.wait_ge(sem, value)
    eng.sem_inc(scratch, 1)


def column(ap, width):
    return ap.unsqueeze(2).to_broadcast([ap.shape[0], ap.shape[1], width])


def middle(ap, count):
    return ap.unsqueeze(1).to_broadcast([ap.shape[0], count, ap.shape[1]])


class Stage:

    def __init__(self, nc, ctx, sems, name):
        self.nc, self.ctx, self.sems, self.name = nc, ctx, sems, name

    def sb(self, name, shape, dt=FP32):
        return self.ctx.enter_context(self.nc.sbuf_tensor(f"{self.name}_{name}", shape, dt))

    def ps(self, name, shape, dt=FP32):
        return self.ctx.enter_context(self.nc.psum_tensor(f"{self.name}_{name}", shape, dt))

    def sem(self, name):
        return self.sems.enter_context(self.nc.semaphore(f"{self.name}_{name}"))

    def block(self):
        return self.ctx.enter_context(self.nc.Block())


def constants(nc, ctx, sems):
    st = Stage(nc, ctx, sems, "const")
    k = {
        "ident": st.sb("ident", [P, P]),
        "iota": st.sb("iota", [P, P]),
        "iota_p": st.sb("iota_p", [P, 1]),
        "eps": st.sb("eps", [P, 1]),
    }
    zeroed, counted = st.sem("zeroed"), st.sem("counted")
    with ExitStack() as inner:
        block = inner.enter_context(nc.Block())

        @block.gpsimd
        def _(pool):
            nc.gpsimd.memset(k["ident"][:, :], 0.0).then_inc(zeroed, 1)
            nc.gpsimd.memset(k["eps"][:, :], LN_EPS)
            nc.gpsimd.iota(k["iota"][:, :], pattern=[[1, P]], base=0, channel_multiplier=0,
                           allow_small_or_imprecise_dtypes=True)
            nc.gpsimd.iota(k["iota_p"][:, :], pattern=[[0, 1]], base=0, channel_multiplier=1,
                           allow_small_or_imprecise_dtypes=True)
            pool.wait_ge(zeroed, 1)
            nc.gpsimd.affine_select(out=k["ident"][:, :], in_=k["ident"][:, :], compare_op=ALU.not_equal,
                                    fill=1.0, base=0, pattern=[[-1, P]], channel_multiplier=1).then_inc(counted, 1)
    return k


def project_heads(nc, sems, k, x, w_heads, b_heads, a_heads, table1, s_src1):
    with ExitStack() as ctx:
        st = Stage(nc, ctx, sems, "proj")
        x_raw = st.sb("x_raw", [P, CHUNK_BLOCKS, FEAT])
        centred = st.sb("centred", [P, CHUNK_BLOCKS, FEAT])
        squares = st.sb("squares", [P, CHUNK_BLOCKS, FEAT])
        normed = st.sb("normed", [P, CHUNK_BLOCKS, FEAT])
        mean = st.sb("mean", [P, CHUNK_BLOCKS])
        spread = st.sb("spread", [P, CHUNK_BLOCKS])
        w_rows = st.sb("w_rows", [P, HD // P, FEAT])
        w_t = st.sb("w_t", [P, FEAT // P, HD])
        a_cols = st.sb("a_cols", [P, HD // P, 2 * HEADS])
        wa = st.sb("wa", [P, FEAT // P, 2 * HEADS])
        b_col = st.sb("b_col", [P, HD // P])
        b_wide = st.sb("b_wide", [P, HD // P, P])
        b_row = st.sb("b_row", [P, HD])
        ba_row = st.sb("ba_row", [P, 2 * HEADS])
        normed_t = st.sb("normed_t", [P, 2, FEAT])
        rows = st.sb("rows", [P, 2, ROW1])
        ps_t = st.ps("ps_t", [P, 2, 512])
        ps_h = st.ps("ps_h", [P, 2, 512])
        ps_s = st.ps("ps_s", [P, 2, 512])

        w_loaded, b_loaded, a_zeroed, a_loaded = (st.sem(n) for n in ("w_loaded", "b_loaded", "a_zeroed", "a_loaded"))
        x_loaded, vec, is_centred, is_squared, std_ready = (
            st.sem(n) for n in ("x_loaded", "vec", "is_centred", "is_squared", "std_ready"))
        var_ready, is_normed, b_widened = st.sem("var_ready"), st.sem("is_normed"), st.sem("b_widened")
        w_turned, w_kept, wa_made, wa_kept = (st.sem(n) for n in ("w_turned", "w_kept", "wa_made", "wa_kept"))
        turned, turn_kept, products, rows_made = (st.sem(n) for n in ("turned", "turn_kept", "products", "rows_made"))
        pool_held = st.sem("pool_held")
        stored = [st.sem("stored0"), st.sem("stored1")]
        VEC = 3
        block = st.block()

        def both(eng, chunk):
            with eng.Fori(0, CHUNKS - 1) as c:
                chunk(c)
            chunk(CHUNKS - 1)

        @block.sync
        def _(sp):
            flat_w = w_heads.rearrange("h d f -> (h d) f").rearrange("(q p) f -> p q f", p=P)
            flat_b = b_heads.rearrange("h d -> (h d)")
            sp.dma_start(w_rows[:, :, :], flat_w).then_inc(w_loaded, 16)
            sp.dma_start(b_col[:, :], flat_b.rearrange("(q p) -> p q", p=P),
                         allow_slow_non_contiguous=True).then_inc(b_loaded, 16)
            sp.dma_start(b_row[:, :], flat_b.partition_broadcast(P)).then_inc(b_loaded, 16)
            sp.wait_ge(a_zeroed, 1)
            for h in range(HEADS):
                at = slice(h % 2 * HDIM, h % 2 * HDIM + HDIM)
                for side in range(2):
                    column_of = side * HEADS + h
                    sp.dma_start(a_cols[at, h // 2, column_of:column_of + 1],
                                 a_heads[h, side * HDIM:(side + 1) * HDIM].unsqueeze(1),
                                 allow_slow_non_contiguous=True).then_inc(a_loaded, 16)
            for s in stored:
                sp.sem_inc(s, 16)

            def chunk(c):
                last = isinstance(c, int)
                for b in range(CHUNK_BLOCKS):
                    sp.wait_ge(rows_made, c * CHUNK_BLOCKS + b + 1)
                    n = LAST if last and b == CHUNK_BLOCKS - 1 else P
                    first = c * (CHUNK_BLOCKS * P) + b * P
                    at = slice(first, first + n) if last else bass.ds(first, n)
                    sp.dma_start(table1[at, :], rows[0:n, b % 2, :]).then_inc(stored[b % 2], 16)
            both(sp, chunk)
            for half, uses in ((0, CHUNKS * 4), (1, CHUNKS * 3)):
                sp.wait_ge(stored[half], 16 * (uses + 1))

        @block.gpsimd
        def _(pool):
            nc.gpsimd.dma_start(x_raw[:, :, :], x[0:CHUNK_BLOCKS * P, :]
                                .rearrange("(b p) f -> p b f", p=P)).then_inc(x_loaded, 16)
            nc.gpsimd.memset(a_cols[:, :, :], 0.0).then_inc(a_zeroed, 1)
            with pool.Fori(0, CHUNKS - 2) as c:
                hold(pool, is_centred, c + 1, pool_held)
                nc.gpsimd.dma_start(x_raw[:, :, :], x[bass.ds((c + 1) * (CHUNK_BLOCKS * P), CHUNK_BLOCKS * P), :]
                                    .rearrange("(b p) f -> p b f", p=P)).then_inc(x_loaded, 16)
            pool.wait_ge(is_centred, CHUNKS - 1)
            tail = (CHUNKS - 1) * CHUNK_BLOCKS * P
            full = (CHUNK_BLOCKS - 1) * P
            nc.gpsimd.dma_start(x_raw[:, 0:CHUNK_BLOCKS - 1, :],
                                x[tail:tail + full, :].rearrange("(b p) f -> p b f", p=P)).then_inc(x_loaded, 16)
            nc.gpsimd.dma_start(x_raw[0:LAST, CHUNK_BLOCKS - 1, :], x[tail + full:NODES, :]).then_inc(x_loaded, 16)

        @block.vector
        def _(dve):
            dve.wait_ge(b_loaded, 32)
            nc.vector.tensor_copy(b_wide[:, :, :], column(b_col[:, :], P)).then_inc(b_widened, 1)
            dve.wait_ge(wa_kept, 1)

            def chunk(c):
                last = isinstance(c, int)
                seq = Chain(dve, vec, c * VEC)
                dve.wait_ge(x_loaded, 16 * (CHUNKS + 1) if last else c * 16 + 16)
                seq.mark(nc.vector.tensor_reduce(mean[:, :], x_raw[:, :, :], AX.X, ALU.add))
                seq.wait()
                seq.mark(nc.vector.tensor_scalar(mean[:, :], mean[:, :], 1.0 / FEAT, None, ALU.mult))
                seq.wait()
                nc.vector.tensor_tensor(centred[:, :, :], x_raw[:, :, :], column(mean[:, :], FEAT),
                                        ALU.subtract).then_inc(is_centred, 1)
                dve.wait_ge(is_squared, c + 1)
                nc.vector.tensor_reduce(spread[:, :], squares[:, :, :], AX.X, ALU.add).then_inc(var_ready, 1)
                dve.wait_ge(std_ready, c + 1)
                seq.mark(nc.vector.reciprocal(spread[:, :], spread[:, :]))
                seq.wait()
                nc.vector.tensor_tensor(normed[:, :, :], centred[:, :, :], column(spread[:, :], FEAT),
                                        ALU.mult).then_inc(is_normed, 1)
                for b in range(CHUNK_BLOCKS):
                    g = c * CHUNK_BLOCKS + b
                    dve.wait_ge(products, g + 1)
                    use = c * (4 if b % 2 == 0 else 3) + b // 2
                    dve.wait_ge(stored[b % 2], use * 16 + 16)
                    nc.vector.tensor_tensor(rows[:, b % 2, 0:HD], ps_h[:, b % 2, :], b_row[:, :], ALU.add)
                    nc.vector.tensor_tensor(rows[:, b % 2, HD:ROW1], ps_s[:, b % 2, HEADS:2 * HEADS],
                                            ba_row[:, HEADS:2 * HEADS], ALU.add)
                    at = g if last else bass.ds(g, 1)
                    out = s_src1[:, at, :] if last else s_src1[:, at, :].rearrange("p o h -> p (o h)")
                    nc.vector.tensor_tensor(out, ps_s[:, b % 2, 0:HEADS], ba_row[:, 0:HEADS],
                                            ALU.add).then_inc(rows_made, 1)
                assert seq.n == VEC
            both(dve, chunk)

        @block.scalar
        def _(act):
            act.wait_ge(w_turned, 1)
            for f in range(FEAT // P):
                nc.scalar.activation(w_t[:, f, :], ps_h[:, f, :], ACT.Copy).then_inc(w_kept, 1)
            act.wait_ge(wa_made, 1)
            for f in range(FEAT // P):
                nc.scalar.activation(wa[:, f, :], ps_s[:, f, 0:2 * HEADS], ACT.Copy)
            nc.scalar.activation(ba_row[:, :], ps_t[:, 0, 0:2 * HEADS], ACT.Copy).then_inc(wa_kept, 1)

            def chunk(c):
                act.wait_ge(is_centred, c + 1)
                nc.scalar.activation(squares[:, :, :], centred[:, :, :], ACT.Square).then_inc(is_squared, 1)
                act.wait_ge(var_ready, c + 1)
                nc.scalar.activation(spread[:, :], spread[:, :], ACT.Sqrt, bias=k["eps"][:, :],
                                     scale=1.0 / FEAT).then_inc(std_ready, 1)
                for b in range(CHUNK_BLOCKS):
                    g = c * CHUNK_BLOCKS + b
                    act.wait_ge(turned, g + 1)
                    nc.scalar.activation(normed_t[:, b % 2, :], ps_t[:, b % 2, 0:FEAT], ACT.Copy).then_inc(turn_kept, 1)
            both(act, chunk)

        @block.tensor
        def _(pe):
            pe.wait_ge(w_loaded, 16)
            for f in range(FEAT // P):
                for q in range(HD // P):
                    ins = nc.tensor.transpose(ps_h[:, f, q * P:(q + 1) * P], w_rows[:, q, f * P:(f + 1) * P], k["ident"][:, :])
            ins.then_inc(w_turned, 1)
            pe.wait_ge(a_loaded, 16 * 2 * HEADS)
            for f in range(FEAT // P):
                for q in range(HD // P):
                    nc.tensor.matmul(ps_s[:, f, 0:2 * HEADS], w_rows[:, q, f * P:(f + 1) * P], a_cols[:, q, :],
                                     start=q == 0, stop=q == HD // P - 1)
            pe.wait_ge(b_widened, 1)
            for q in range(HD // P):
                ins = nc.tensor.matmul(ps_t[:, 0, 0:2 * HEADS], b_wide[:, q, :], a_cols[:, q, :],
                                       start=q == 0, stop=q == HD // P - 1)
            ins.then_inc(wa_made, 1)
            pe.wait_ge(w_kept, FEAT // P)
            pe.wait_ge(wa_kept, 1)

            def chunk(c):
                pe.wait_ge(is_normed, c + 1)

                def turn(b):
                    for f in range(FEAT // P):
                        ins = nc.tensor.transpose(ps_t[:, b % 2, f * P:(f + 1) * P], normed[:, b, f * P:(f + 1) * P],
                                                  k["ident"][:, :])
                    ins.then_inc(turned, 1)

                turn(0)
                for b in range(CHUNK_BLOCKS):
                    g = c * CHUNK_BLOCKS + b
                    pe.wait_ge(turn_kept, g + 1)
                    if b >= 2:
                        pe.wait_ge(rows_made, g - 1)
                    if b + 1 < CHUNK_BLOCKS:
                        turn(b + 1)
                    for f in range(FEAT // P):
                        nc.tensor.matmul(ps_h[:, b % 2, :], normed_t[:, b % 2, f * P:(f + 1) * P], w_t[:, f, :],
                                         start=f == 0, stop=f == FEAT // P - 1)
                    for f in range(FEAT // P):
                        ins = nc.tensor.matmul(ps_s[:, b % 2, 0:2 * HEADS], normed_t[:, b % 2, f * P:(f + 1) * P],
                                               wa[:, f, :], start=f == 0, stop=f == FEAT // P - 1)
                    ins.then_inc(products, 1)
            both(pe, chunk)


def sort_edges(nc, sems, k, src, dst, node_of, local_of, step_info):
    with ExitStack() as ctx:
        st = Stage(nc, ctx, sems, "sort")
        src_i, dst_i = st.sb("src_i", [EP, ECOLS], I32), st.sb("dst_i", [EP, ECOLS], I32)
        scratch_i = st.sb("scratch_i", [EP, ECOLS], I32)
        key = st.sb("key", [EP, ECOLS], BF16)
        low, high = st.sb("low", [EP, ECOLS]), st.sb("high", [EP, ECOLS])
        place = st.sb("place", [EP, PARTS, PCOLS])
        lane, tile = (src_i[:, n * PCOLS:(n + 1) * PCOLS].bitcast(FP32) for n in range(2))
        place_i = src_i[:, 2 * PCOLS:3 * PCOLS]
        member_all = st.sb("member", [P, BLOCKS * PCOLS], BF16)
        member = member_all[0:EP, :]
        mask = st.sb("mask", [EP, 2, PCOLS], U16)
        before = st.sb("before", [P, P])
        before_b = st.sb("before_b", [EP, P], BF16)
        step_back = st.sb("step_back", [P, P])
        one_column = st.sb("one_column", [EP, 2 * P], BF16)
        row_of = st.sb("row_of", [P, BLOCKS, P], BF16)
        zeros_b = st.sb("zeros_b", [P, PHALF], BF16)
        zeros_h = st.sb("zeros_h", [EP, THALF], FP16)
        ones = st.sb("ones", [P, PCOLS])
        one_each = st.sb("one_each", [P, 1])
        counted_blocks = st.sb("counted_blocks", [P, 1])
        far = st.sb("far", [P, 1])
        total = st.sb("total", [P, PCOLS])
        upto = st.sb("upto", [P, PCOLS])
        start_hi, start_lo = st.sb("start_hi", [P, PCOLS], BF16), st.sb("start_lo", [P, PCOLS], BF16)
        count_i = st.sb("count_i", [P, 1], I32)
        tiles = st.sb("tiles", [P, PARTS])
        tiles_all = st.sb("tiles_all", [P, 1])
        first_tile = st.sb("first_tile", [P, PARTS])
        first_edge = st.sb("first_edge", [P, 1])
        first_step = st.sb("first_step", [P, PARTS])
        shift = st.sb("shift", [P, PARTS])
        shift_step = st.sb("shift_step", [P, PARTS])
        count_tiles = st.sb("count_tiles", [P, STEPS])
        count_tiles_h = st.sb("count_tiles_h", [EP, PART_TILES], FP16)
        lanes_h = st.sb("lanes_h", [EP, P], FP16)
        SLOTS = 5
        by_lane = st.sb("by_lane", [EP, SLOTS, 2, P], FP16)
        by_tile = st.sb("by_tile", [EP, SLOTS, PART_TILES], FP16)
        high_sb = st.sb("high_sb", [P, PART_TILES])
        packed = st.sb("packed", [P, PART_TILES])
        TB = -(-PART_TILES // P)
        packed_t = st.sb("packed_t", [P, PARTS, TB, P])
        reached = st.sb("reached", [P, PART_TILES])
        step_of = st.sb("step_of", [P, PARTS * TB])
        QUARTER = STEPS // 4

        def later(row, rows, dt):
            at = member_all[:, row * 2 * STEPS:(row + rows) * 2 * STEPS]
            return at.bitcast(dt).rearrange("p (r s) -> p r s", r=rows)
        goes_to = later(0, 2, FP32)
        final_i, part_i, part2_i = (later(r, 1, I32)[:, 0, :] for r in (2, 3, 4))
        flags = later(5, 2, FP32)[0:1, :, :]
        nowhere = goes_to[0:1, 0, :]
        block_row = st.sb("block_row", [1, STEPS + 2])
        bank_i, row_tmp = final_i[0:1, :], count_tiles[0:1, :]
        bank_row = part_i[0:1, :].bitcast(FP32)

        names = ("loaded zeroed shaped vec is_member counted totals_out placed_start ranked rank_used prefixed "
                 "numbered slot_made slot_used swept high_out packed_made packed_turned turn_out reach_made step_made "
                 "step_known route_made route_used block_known row_cleared cast masked held held_pe")
        s = {n: st.sem(n) for n in names.split()}
        ps_a, ps_b = st.ps("ps_a", [P, 2, 512]), st.ps("ps_b", [P, 2, 512])
        ps_c, ps_d = st.ps("ps_c", [P, 2, 512]), st.ps("ps_d", [P, 2, 512])
        block = st.block()

        @block.sync
        def _(sp):
            sp.dma_start(src_i[:, :], src.rearrange("(p t) -> p t", p=EP)).then_inc(s["loaded"], 16)
            sp.dma_start(dst_i[:, :], dst.rearrange("(p t) -> p t", p=EP)).then_inc(s["loaded"], 16)

        @block.gpsimd
        def _(pool):
            exact = {"allow_small_or_imprecise_dtypes": True}
            nc.gpsimd.memset(before[:, :], 1.0).then_inc(s["zeroed"], 1)
            nc.gpsimd.memset(one_column[:, :], 0.0).then_inc(s["zeroed"], 1)
            nc.gpsimd.memset(one_each[:, :], 1.0).then_inc(s["zeroed"], 1)
            nc.gpsimd.memset(far[:, :], 0.0).then_inc(s["zeroed"], 1)
            nc.gpsimd.memset(zeros_b[:, :], 0.0)
            nc.gpsimd.memset(zeros_h[:, :], 0.0)
            nc.gpsimd.memset(ones[:, :], 1.0)
            nc.gpsimd.iota(count_tiles[:, :], pattern=[[1, STEPS]], base=0, channel_multiplier=0, **exact)
            nc.gpsimd.iota(count_tiles_h[:, :], pattern=[[1, PART_TILES]], base=0, channel_multiplier=0, **exact)
            nc.gpsimd.iota(lanes_h[:, :], pattern=[[1, P]], base=0, channel_multiplier=0, **exact)
            pool.wait_ge(s["zeroed"], 4)
            nc.gpsimd.affine_select(out=before[:, :], in_=before[:, :], compare_op=ALU.is_gt, fill=0.0, base=0,
                                    pattern=[[1, P]], channel_multiplier=-1)
            nc.gpsimd.affine_select(out=step_back[:, :], in_=k["ident"][:, :], compare_op=ALU.not_equal, fill=-1.0,
                                    base=-1, pattern=[[1, P]], channel_multiplier=-1)
            nc.gpsimd.affine_select(out=one_column[:, :], in_=one_column[:, :], compare_op=ALU.not_equal, fill=1.0,
                                    base=-P, pattern=[[1, 2 * P]], channel_multiplier=0)
            nc.gpsimd.affine_select(out=one_each[:, :], in_=one_each[:, :], compare_op=ALU.is_gt, fill=0.0,
                                    base=BLOCKS, pattern=[[0, 1]], channel_multiplier=-1)
            nc.gpsimd.affine_select(out=far[:, :], in_=far[:, :], compare_op=ALU.not_equal, fill=NOWHERE,
                                    base=-BLOCKS, pattern=[[0, 1]], channel_multiplier=1).then_inc(s["shaped"], 1)
            pool.wait_ge(s["shaped"], 1)
            nc.gpsimd.affine_select(out=counted_blocks[:, :], in_=one_each[:, :], compare_op=ALU.is_gt, fill=0.0,
                                    base=0, pattern=[[0, 1]], channel_multiplier=1).then_inc(s["shaped"], 1)
            pool.wait_ge(s["route_used"], PARTS * TB)
            nc.gpsimd.iota(nowhere[:, :], pattern=[[0, STEPS // 2], [1, 2]], base=BLOCKS, channel_multiplier=0, **exact)\
                .then_inc(s["shaped"], 1)

        @block.vector
        def _(dve):
            seq = Chain(dve, s["vec"])
            dve.wait_ge(s["shaped"], 2)
            nc.vector.tensor_copy(before_b[:, :], before[0:EP, :]).then_inc(s["cast"], 1)
            nc.vector.tensor_copy(row_of[:, :, :], column(k["ident"][:, 0:BLOCKS], P)).then_inc(s["cast"], 1)
            dve.wait_ge(s["loaded"], 32)
            seq.mark(nc.vector.tensor_scalar(scratch_i[:, :], src_i[:, :], 7, None, ALU.logical_shift_right))
            seq.wait()
            seq.mark(nc.vector.tensor_copy(key[:, :], scratch_i[:, :]))
            seq.wait()
            seq.mark(nc.vector.tensor_scalar(scratch_i[:, :], dst_i[:, :], DST_LOW - 1, None, ALU.bitwise_and))
            seq.wait()
            seq.mark(nc.vector.tensor_copy(low[:, :], scratch_i[:, :]))
            seq.wait()
            seq.mark(nc.vector.tensor_scalar(scratch_i[:, :], dst_i[:, :], 10, None, ALU.logical_shift_right))
            seq.wait()
            seq.mark(nc.vector.tensor_scalar(high[:, :], scratch_i[:, :], float(P), float(P), ALU.mult, ALU.add))
            seq.wait()
            seq.mark(nc.vector.tensor_scalar(scratch_i[:, :], src_i[:, :], P - 1, None, ALU.bitwise_and))
            seq.wait()
            seq.mark(nc.vector.tensor_tensor(high[:, :], high[:, :], scratch_i[:, :], ALU.add))
            seq.wait()

            for part in range(PARTS):
                cols = slice(part * PCOLS, (part + 1) * PCOLS)
                if part:
                    dve.wait_ge(s["ranked"], part * BLOCKS)
                with dve.Fori(0, BLOCKS) as b:
                    nc.vector.tensor_scalar(member[:, bass.ds(b * PCOLS, PCOLS)], key[:, cols],
                                            k["iota"][0:EP, bass.ds(b, 1)], None, ALU.is_equal).then_inc(s["is_member"], 1)
                dve.wait_ge(s["totals_out"], 2 * (part + 1))
                seq.mark(nc.vector.tensor_tensor_scan(upto[:, :], ones[:, :], total[:, :], 0.0, ALU.mult, ALU.add))
                seq.wait()
                seq.mark(nc.vector.tensor_scalar(count_i[:, :], upto[:, PCOLS - 1:PCOLS], float(P - 1), None, ALU.add))
                seq.wait()
                seq.mark(nc.vector.tensor_scalar(count_i[:, :], count_i[:, :], 7, None, ALU.arith_shift_right))
                seq.wait()
                at = tiles[:, part:part + 1]
                if part == 0:
                    nc.vector.tensor_tensor(at, count_i[:, :], one_each[:, :], ALU.max).then_inc(s["counted"], 1)
                else:
                    nc.vector.tensor_copy(at, count_i[:, :]).then_inc(s["counted"], 1)
                seq.mark(nc.vector.tensor_tensor(upto[:, :], upto[:, :], total[:, :], ALU.subtract))
                dve.wait_ge(s["prefixed"], part + 1)
                seq.mark(nc.vector.tensor_copy(first_tile[:, part:part + 1], ps_a[:, 0, 0:1]))
                seq.wait()
                seq.mark(nc.vector.tensor_scalar(first_edge[:, :], first_tile[:, part:part + 1], float(P), None, ALU.mult))
                seq.wait()
                seq.mark(nc.vector.tensor_scalar(upto[:, :], upto[:, :], first_edge[:, :], None, ALU.add))
                seq.wait()
                seq.mark(nc.vector.tensor_scalar(total[:, :], upto[:, :], 1.0 / 512, MAGIC, ALU.mult, ALU.add))
                seq.wait()
                seq.mark(nc.vector.tensor_scalar(start_hi[:, :], total[:, :], -MAGIC, 512.0, ALU.add, ALU.mult))
                seq.wait()
                nc.vector.tensor_tensor(start_lo[:, :], upto[:, :], start_hi[:, :], ALU.subtract)\
                    .then_inc(s["placed_start"], 1)
                here = place[:, part, :].rearrange("p (h t) -> p h t", h=2)

                def take(b, ps, slot, turn):
                    which = k["iota"][0:EP, b:b + 1] if isinstance(b, int) else k["iota"][0:EP, bass.ds(b, 1)]
                    nc.vector.tensor_scalar(mask[:, slot, :], key[:, cols], which, None, ALU.is_equal).then_inc(s["masked"], 1)
                    hold(dve, s["ranked"], turn + 1, s["held"])
                    hold(dve, s["masked"], turn + 1, s["held"])
                    nc.vector.copy_predicated(here, mask[:, slot, :].rearrange("p (h t) -> p h t", h=2),
                                              ps[0:EP, :, 0:PHALF]).then_inc(s["rank_used"], 1)
                with dve.Fori(0, BLOCKS // 2) as i:
                    take(i * 2, ps_b, 0, i * 2 + part * BLOCKS)
                    take(i * 2 + 1, ps_c, 1, i * 2 + 1 + part * BLOCKS)
                take(BLOCKS - 1, ps_b, 0, BLOCKS - 1 + part * BLOCKS)

            seq.mark(nc.vector.tensor_tensor(tiles_all[:, :], tiles[:, 0:1], tiles[:, 1:2], ALU.add))
            seq.wait()
            nc.vector.tensor_tensor(tiles_all[:, :], tiles_all[:, :], tiles[:, 2:3], ALU.add).then_inc(s["counted"], 1)
            dve.wait_ge(s["prefixed"], PARTS + 1)
            seq.mark(nc.vector.tensor_copy(first_step[:, 0:1], ps_a[:, 0, 0:1]))
            seq.wait()
            for part in range(1, PARTS):
                seq.mark(nc.vector.tensor_tensor(first_step[:, part:part + 1], first_step[:, part - 1:part],
                                                 tiles[:, part - 1:part], ALU.add))
                seq.wait()
            nc.vector.tensor_tensor(shift[:, :], first_step[:, :], first_tile[:, :], ALU.subtract).then_inc(s["counted"], 1)
            dve.wait_ge(s["prefixed"], PARTS + 2)
            seq.mark(nc.vector.tensor_tensor(shift_step[:, :], ps_a[:, 0, 0:PARTS], far[:, :].to_broadcast([P, PARTS]), ALU.add))
            seq.wait()
            nc.vector.tensor_scalar(goes_to[:, 0, :], count_tiles[:, :], first_step[:, 0:1], None, ALU.is_ge)\
                .then_inc(s["counted"], 1)

            for part in range(PARTS):
                seq.mark(nc.vector.tensor_copy(place_i[:, :], place[:, part, :]))
                seq.wait()
                seq.mark(nc.vector.tensor_scalar(scratch_i[:, 0:PCOLS], place_i[:, :], P - 1, None, ALU.bitwise_and))
                seq.mark(nc.vector.tensor_scalar(place_i[:, :], place_i[:, :], 7, None, ALU.logical_shift_right))
                seq.wait()
                seq.mark(nc.vector.tensor_copy(lane[:, :], scratch_i[:, 0:PCOLS]))
                seq.mark(nc.vector.tensor_copy(tile[:, :], place_i[:, :]))
                seq.wait()
                with dve.Fori(0, PCOLS // (2 * SLOTS)) as i:
                    for j in range(2 * SLOTS):
                        n = i * (2 * SLOTS) + j
                        slot = j % SLOTS
                        at = bass.ds(n, 1)
                        value_at = bass.ds(n + part * PCOLS, 1)
                        dve.wait_ge(s["slot_used"], n + part * PCOLS + 1)
                        nc.vector.tensor_scalar(by_lane[:, slot, 0, :], lanes_h[:, :], lane[:, at], low[:, value_at],
                                                ALU.is_equal, ALU.mult)
                        nc.vector.tensor_scalar(by_lane[:, slot, 1, :], lanes_h[:, :], lane[:, at], high[:, value_at],
                                                ALU.is_equal, ALU.mult)
                        nc.vector.tensor_scalar(by_tile[:, slot, :], count_tiles_h[:, :], tile[:, at], None, ALU.is_equal)\
                            .then_inc(s["slot_made"], 1)
                dve.wait_ge(s["high_out"], part + 1)
                if part:
                    dve.wait_ge(s["packed_turned"], part * TB)
                nc.vector.scalar_tensor_tensor(packed[:, :].rearrange("p (h t) -> p h t", h=2),
                                               high_sb[:, :].rearrange("p (h t) -> p h t", h=2), float(DST_LOW),
                                               ps_a[:, :, 0:THALF], ALU.mult, ALU.add).then_inc(s["packed_made"], 1)
                nc.vector.tensor_scalar(reached[:, :], count_tiles[:, 0:PART_TILES], first_tile[:, part:part + 1], None,
                                        ALU.is_ge).then_inc(s["reach_made"], 1)
                dve.wait_ge(s["step_known"], part + 1)
                for t in range(TB):
                    n = part * TB + t
                    w = min(P, PART_TILES - t * P)
                    seq.mark(nc.vector.tensor_scalar(step_of[0:w, n:n + 1], ps_d[0:w, 1, t:t + 1], k["iota_p"][0:w, :],
                                                     float(t * P), ALU.add, ALU.add))
                seq.wait()

            dve.wait_ge(s["step_made"], 1)
            for n in range(PARTS * TB):
                w = min(P, PART_TILES - n % TB * P)
                if n >= 2:
                    dve.wait_ge(s["route_used"], n - 1)
                nc.vector.tensor_scalar(goes_to[0:w, n % 2, :], count_tiles[0:w, :], step_of[0:w, n:n + 1], None,
                                        ALU.is_equal).then_inc(s["route_made"], 1)

            dve.wait_ge(s["route_used"], PARTS * TB)
            seq.mark(nc.vector.tensor_copy(final_i[:, 0:2 * QUARTER].rearrange("p (q t) -> p q t", q=2), ps_a[:, :, 0:QUARTER]))
            seq.mark(nc.vector.tensor_copy(final_i[:, 2 * QUARTER:].rearrange("p (q t) -> p q t", q=2), ps_b[:, :, 0:QUARTER]))
            seq.wait()
            seq.mark(nc.vector.tensor_scalar(part_i[:, :], final_i[:, :], 17, None, ALU.logical_shift_right))
            seq.mark(nc.vector.tensor_scalar(part2_i[:, :], final_i[:, :], DST_LOW - 1, None, ALU.bitwise_and))
            seq.wait()
            seq.mark(nc.vector.tensor_scalar(count_tiles[:, :], part_i[:, :], -1.0, 0.0, ALU.add, ALU.max))
            seq.wait()
            seq.mark(nc.vector.scalar_tensor_tensor(node_of[:, :], count_tiles[:, :], float(DST_LOW), part2_i[:, :],
                                                    ALU.mult, ALU.add))
            seq.wait()
            seq.mark(nc.vector.tensor_scalar(part2_i[:, :], final_i[:, :], 10, P - 1, ALU.logical_shift_right, ALU.bitwise_and))
            seq.mark(nc.vector.tensor_scalar(count_tiles[:, :], part_i[:, :], 0.0, NO_NODE, ALU.is_equal, ALU.mult))
            seq.wait()
            seq.mark(nc.vector.tensor_tensor(local_of[:, :], count_tiles[:, :], part2_i[:, :], ALU.add))
            dve.wait_ge(s["block_known"], 2)
            seq.wait()
            blocks = block_row[:, 1:STEPS + 1]
            seq.mark(nc.vector.tensor_tensor(flags[:, 0, :], blocks, block_row[:, 0:STEPS], ALU.not_equal))
            seq.mark(nc.vector.tensor_tensor(flags[:, 1, :], blocks, block_row[:, 2:STEPS + 2], ALU.not_equal))
            seq.mark(nc.vector.tensor_scalar(bank_row[:, :], blocks, -1.0, 1.0 / SUM_BANKS, ALU.add, ALU.mult))
            seq.wait()
            seq.mark(nc.vector.tensor_scalar(bank_row[:, :], bank_row[:, :], MAGIC, None, ALU.add))
            seq.wait()
            seq.mark(nc.vector.tensor_scalar(bank_row[:, :], bank_row[:, :], -MAGIC, -float(SUM_BANKS), ALU.add, ALU.mult))
            seq.wait()
            seq.mark(nc.vector.tensor_tensor(bank_row[:, :], bank_row[:, :], blocks, ALU.add))
            for_pe = step_info[0:1, :].rearrange("p (s f) -> p s f", f=2)
            for_act = step_info[32:33, :].rearrange("p (s f) -> p s f", f=2)
            seq.mark(nc.vector.tensor_copy(step_info[64:65, 0:STEPS], blocks))
            seq.wait()
            seq.mark(nc.vector.tensor_copy(for_pe[:, :, 0], bank_row[:, :]))
            dve.wait_ge(s["shaped"], 3)
            for info, value, other, flag in ((for_pe[:, :, 1], bank_row[:, :], IDLE_BANK, 0),
                                             (for_act[:, :, 0], bank_row[:, :], SPARE_BANK, 1)):
                seq.mark(nc.vector.scalar_tensor_tensor(row_tmp[:, :], value, -float(other), flags[:, flag, :],
                                                        ALU.add, ALU.mult))
                seq.wait()
                seq.mark(nc.vector.tensor_scalar(info, row_tmp[:, :], float(other), None, ALU.add))
                seq.wait()
            seq.mark(nc.vector.tensor_tensor(row_tmp[:, :], blocks, nowhere, ALU.subtract))
            seq.wait()
            seq.mark(nc.vector.tensor_tensor(row_tmp[:, :], row_tmp[:, :], flags[:, 1, :], ALU.mult))
            seq.wait()
            seq.mark(nc.vector.tensor_tensor(for_act[:, :, 1], row_tmp[:, :], nowhere, ALU.add))

        @block.scalar
        def _(act):
            nc.scalar.activation(block_row[:, :], k["iota"][0:1, 0:1].to_broadcast([1, STEPS + 2]), ACT.Copy, bias=-1.0)\
                .then_inc(s["row_cleared"], 1)
            for part in range(PARTS):
                act.wait_ge(s["numbered"], part + 1)
                for half in range(2):
                    nc.scalar.activation(total[:, half * PHALF:(half + 1) * PHALF], ps_d[:, half, 0:PHALF], ACT.Copy)\
                        .then_inc(s["totals_out"], 1)
            act.wait_ge(s["step_made"], 1)
            act.wait_ge(s["row_cleared"], 1)
            for h, ps in enumerate((ps_c, ps_d)):
                nc.scalar.activation(block_row[:, 1 + 2 * h * QUARTER:1 + 2 * (h + 1) * QUARTER]
                                     .rearrange("p (q t) -> p q t", q=2), ps[0:1, :, 0:QUARTER], ACT.Copy)\
                    .then_inc(s["block_known"], 1)
            for part in range(PARTS):
                act.wait_ge(s["swept"], part + 1)
                if part:
                    act.wait_ge(s["packed_made"], part)
                nc.scalar.activation(high_sb[:, :].rearrange("p (h t) -> p h t", h=2), ps_b[:, :, 0:THALF], ACT.Copy)\
                    .then_inc(s["high_out"], 1)
                for t in range(TB):
                    w = min(P, PART_TILES - t * P)
                    act.wait_ge(s["packed_turned"], part * TB + t + 1)
                    nc.scalar.activation(packed_t[0:w, part, t, :], ps_c[0:w, (part * TB + t) % 2, 0:P], ACT.Copy)\
                        .then_inc(s["turn_out"], 1)

        @block.tensor
        def _(pe):
            pe.sem_inc(s["slot_used"], SLOTS)
            pe.sem_inc(s["rank_used"], 2)
            pe.wait_ge(s["shaped"], 2)
            pe.wait_ge(s["cast"], 2)
            half_of = [slice(h * PHALF, (h + 1) * PHALF) for h in range(2)]

            for part in range(PARTS):
                if part:
                    pe.wait_ge(s["totals_out"], 2 * part)
                for h in range(2):
                    nc.tensor.matmul(ps_d[:, h, 0:PHALF], zeros_b[0:EP, 0:P], zeros_b[0:EP, :], start=True, stop=False)
                with pe.Fori(0, BLOCKS) as b:
                    hold(pe, s["is_member"], b + (part * BLOCKS + 1), s["held_pe"])
                    for h in range(2):
                        nc.tensor.matmul(ps_d[:, h, 0:PHALF], one_column[:, bass.ds(P - b, P)],
                                         member[:, bass.ds(b * PCOLS + h * PHALF, PHALF)], start=False, stop=False)
                for h in range(2):
                    ins = nc.tensor.matmul(ps_d[:, h, 0:PHALF], zeros_b[0:EP, 0:P], zeros_b[0:EP, :], start=False, stop=True)
                ins.then_inc(s["numbered"], 1)
                pe.wait_ge(s["counted"], part + 1)
                nc.tensor.matmul(ps_a[:, 0, 0:1], before[:, :], tiles[:, part:part + 1], start=True, stop=True)\
                    .then_inc(s["prefixed"], 1)
                pe.wait_ge(s["placed_start"], part + 1)
                if part:
                    pe.wait_ge(s["rank_used"], part * BLOCKS + 2)

                def rank(b, ps, turn):
                    hold(pe, s["rank_used"], turn + 1, s["held_pe"])
                    for h in range(2):
                        off = b * PCOLS + h * PHALF
                        here = member[:, off:off + PHALF] if isinstance(b, int) else member[:, bass.ds(off, PHALF)]
                        row = row_of[:, b, :] if isinstance(b, int) else \
                            row_of[:, bass.ds(b, 1), :].rearrange("p o j -> p (o j)")
                        nc.tensor.matmul(ps[:, h, 0:PHALF], before_b[:, :], here, start=True, stop=False)
                        nc.tensor.matmul(ps[:, h, 0:PHALF], row, start_hi[:, half_of[h]], start=False, stop=False)
                        ins = nc.tensor.matmul(ps[:, h, 0:PHALF], row, start_lo[:, half_of[h]], start=False, stop=True)
                    ins.then_inc(s["ranked"], 1)
                with pe.Fori(0, BLOCKS // 2) as i:
                    rank(i * 2, ps_b, i * 2 + part * BLOCKS)
                    rank(i * 2 + 1, ps_c, i * 2 + 1 + part * BLOCKS)
                rank(BLOCKS - 1, ps_b, BLOCKS - 1 + part * BLOCKS)

            pe.wait_ge(s["counted"], PARTS + 1)
            nc.tensor.matmul(ps_a[:, 0, 0:1], before[:, :], tiles_all[:, :], start=True, stop=True).then_inc(s["prefixed"], 1)
            pe.wait_ge(s["counted"], PARTS + 2)
            nc.tensor.matmul(ps_a[:, 0, 0:PARTS], step_back[:, :], shift[:, :], start=True, stop=True)\
                .then_inc(s["prefixed"], 1)
            pe.wait_ge(s["counted"], PARTS + 3)
            for q in range(4):
                ins = nc.tensor.matmul((ps_c, ps_d)[q // 2][0:1, q % 2, 0:QUARTER], counted_blocks[:, :],
                                       goes_to[:, 0, q * QUARTER:(q + 1) * QUARTER], start=True, stop=True)
            ins.then_inc(s["step_made"], 1)

            for part in range(PARTS):
                if part:
                    pe.wait_ge(s["packed_made"], part)
                    pe.wait_ge(s["high_out"], part)
                for ps in (ps_a, ps_b):
                    for h in range(2):
                        nc.tensor.matmul(ps[:, h, 0:THALF], zeros_h[:, 0:P], zeros_h[:, :], start=True, stop=False)
                with pe.Fori(0, PCOLS // (2 * SLOTS)) as i:
                    for j in range(2 * SLOTS):
                        slot = j % SLOTS
                        pe.wait_ge(s["slot_made"], i * (2 * SLOTS) + (part * PCOLS + j + 1))
                        for number, ps in enumerate((ps_a, ps_b)):
                            for h in range(2):
                                ins = nc.tensor.matmul(ps[:, h, 0:THALF], by_lane[:, slot, number, :],
                                                       by_tile[:, slot, h * THALF:(h + 1) * THALF], start=False, stop=False)
                        ins.then_inc(s["slot_used"], 1)
                for ps in (ps_a, ps_b):
                    for h in range(2):
                        ins = nc.tensor.matmul(ps[:, h, 0:THALF], zeros_h[:, 0:P], zeros_h[:, :], start=False, stop=True)
                ins.then_inc(s["swept"], 1)
                pe.wait_ge(s["packed_made"], part + 1)
                if part == 0:
                    pe.wait_ge(s["block_known"], 2)
                for t in range(TB):
                    n = part * TB + t
                    w = min(P, PART_TILES - t * P)
                    if n >= 2:
                        pe.wait_ge(s["turn_out"], n - 1)
                    nc.tensor.transpose(ps_c[0:w, n % 2, 0:P], packed[:, t * P:t * P + w], k["ident"][:, :])\
                        .then_inc(s["packed_turned"], 1)
                pe.wait_ge(s["reach_made"], part + 1)
                for t in range(TB):
                    w = min(P, PART_TILES - t * P)
                    ins = nc.tensor.matmul(ps_d[0:w, 1, t:t + 1], reached[:, t * P:t * P + w], shift_step[:, part:part + 1],
                                           start=True, stop=True)
                ins.then_inc(s["step_known"], 1)

            pe.wait_ge(s["turn_out"], PARTS * TB)
            for n in range(PARTS * TB):
                w = min(P, PART_TILES - n % TB * P)
                pe.wait_ge(s["route_made"], n + 1)
                for q in range(4):
                    ins = nc.tensor.matmul((ps_a, ps_b)[q // 2][:, q % 2, 0:QUARTER], packed_t[0:w, n // TB, n % TB, :],
                                           goes_to[0:w, n % 2, q * QUARTER:(q + 1) * QUARTER],
                                           start=n == 0, stop=n == PARTS * TB - 1)
                ins.then_inc(s["route_used"], 1)


TURN_AT, KEEP_AT, WEIGH_AT, SCORES_AT = 0, 1, 2, 3


def aggregate(nc, sems, k, name, table, row, width, heads, s_src, node_of, local_of, step_info, sums_of, loads=()):
    with ExitStack() as ctx:
        st = Stage(nc, ctx, sems, name)
        rows = st.sb("rows", [P, RING, GROUP, row])
        target = st.sb("target", [P, RING, GROUP], I32)
        hot = st.sb("hot", [P, RING, GROUP, P])
        hot_t = st.sb("hot_t", [P, GROUP, P])
        score = st.sb("score", [P, 2, GROUP, heads])
        weight = st.sb("weight", [P, 2, GROUP, heads])
        weighted_hot = st.sb("weighted_hot", [P, 2, GROUP, P]) if heads == 1 else None
        zeros = st.sb("zeros", [P, 512], BF16)
        banks = st.ps("banks", [P, (SUM_BANKS + 2) * 512])
        ps_t = st.ps("ps_t", [P, GROUP, P])
        ps_s = st.ps("ps_s", [P, 2, 512])
        names = ("zeroed target_ready held_pool held_act is_hot turned turn_kept scored added leaky is_weight ready "
                 "summed taken loaded")
        s = {n: st.sem(n) for n in names.split()}
        gathered = [st.sem(f"gathered{u}") for u in range(RING)]
        FREE = RING * GROUP
        block = st.block()

        def rounds(eng, body):
            with eng.Fori(0, ROUNDS) as r:
                for u in range(RING):
                    body(r * RING + u, r, u)
            for g in range(ROUNDS * RING, GROUPS):
                body(g, g // RING, g % RING)

        def exists(g, ahead):
            return not isinstance(g, int) or g + ahead < GROUPS

        def cols(at, n):
            return slice(at, at + n) if isinstance(at, int) else bass.ds(at, n)

        @block.sync
        def _(sp):
            for there, here in loads:
                sp.dma_start(there, here).then_inc(s["loaded"], 16)
            if loads:
                sp.wait_ge(s["loaded"], 16 * len(loads))

        @block.gpsimd
        def _(pool):
            def body(g, r, u):
                hold(pool, s["target_ready"], g + 1, s["held_pool"])
                hold(pool, s["summed"], g * GROUP + GROUP, s["held_pool"])
                for j in range(GROUP):
                    nc.gpsimd.indirect_dma_start(
                        out=rows[:, u, j, :], out_offset=None, in_=table[:, :],
                        in_offset=bass.IndirectOffsetOnAxis(ap=target[:, u, j:j + 1], axis=0)).then_inc(gathered[u], 16)
            rounds(pool, body)

        @block.vector
        def _(dve):
            nc.vector.memset(zeros[:, :], 0.0).then_inc(s["zeroed"], 1)

            def copy_targets(g, u):
                nc.vector.tensor_copy(target[:, u, :], node_of[:, cols(g * GROUP, GROUP)]).then_inc(s["target_ready"], 1)

            def make_hot(g, u):
                nc.vector.tensor_tensor(hot[:, u, :, :], middle(k["iota"][:, :], GROUP),
                                        column(local_of[:, cols(g * GROUP, GROUP)], P), ALU.is_equal).then_inc(s["is_hot"], 1)

            def add_scores(g, r, u):
                dve.wait_ge(s["scored"], g + 1)
                dve.wait_ge(gathered[u], r * (16 * GROUP) + 16 * GROUP)
                nc.vector.tensor_tensor(score[:, u % 2, :, :],
                                        ps_s[:, u % 2, 0:GROUP * heads].rearrange("p (j h) -> p j h", h=heads),
                                        rows[:, u, :, width:width + heads], ALU.add).then_inc(s["added"], 1)
                dve.wait_ge(s["added"], g + 1)
                flat = score[:, u % 2, :, :].rearrange("p j h -> p (j h)")
                nc.vector.scalar_tensor_tensor(flat, flat, SLOPE, flat, ALU.mult, ALU.max).then_inc(s["leaky"], 1)

            for u in range(RING):
                copy_targets(u, u)
            for u in range(3):
                make_hot(u, u)
            add_scores(0, 0, 0)

            def body(g, r, u):
                dve.wait_ge(s["is_weight"], g + 1)
                for j in range(GROUP):
                    if heads == 1:
                        if j == 0:
                            dve.wait_ge(s["summed"], g * GROUP + (FREE - GROUP))
                        nc.vector.tensor_scalar(weighted_hot[:, u % 2, j, :], hot[:, u, j, :], weight[:, u % 2, j, :], None,
                                                ALU.mult).then_inc(s["ready"], 1)
                    else:
                        by_head = rows[:, u, j, 0:width].rearrange("p (h d) -> p h d", h=heads)
                        nc.vector.tensor_tensor(by_head, by_head, column(weight[:, u % 2, j, :], width // heads),
                                                ALU.mult).then_inc(s["ready"], 1)
                if exists(g, 1):
                    add_scores(g + 1, r + (u + 1) // RING, (u + 1) % RING)
                if exists(g, 3):
                    dve.wait_ge(s["summed"], g * GROUP + (FREE - 2 * GROUP))
                    make_hot(g + 3, (u + 3) % RING)
                if exists(g, RING):
                    copy_targets(g + RING, u)
            rounds(dve, body)

        @block.scalar
        def _(act):
            act.sem_inc(s["taken"], SUM_BANKS)

            def keep_turn(g):
                act.wait_ge(s["turned"], g + 1)
                if not (isinstance(g, int) and g == 0):
                    act.wait_ge(s["scored"], g)
                nc.scalar.activation(hot_t[:, :, :], ps_t[:, :, :], ACT.Copy).then_inc(s["turn_kept"], 1)

            def weigh(g, u):
                act.wait_ge(s["leaky"], g + 1)
                nc.scalar.activation(weight[:, u % 2, :, :], score[:, u % 2, :, :], ACT.Exp, scale=-1.0)\
                    .then_inc(s["is_weight"], 1)

            def load_step(step):
                _, (bank, place) = nc.values_load_multi_w_load_instructions(
                    step_info[32:33, cols(step * 2, 2)], engines=(mybir.EngineType.Activation,), min_val=0,
                    max_val=BLOCKS + 1, skip_runtime_bounds_check_because="the sort writes them within bounds")
                return nc.s_assert_within(bank, 0, SPARE_BANK, skip_runtime_bounds_check_because="a bank number"), place

            keep_turn(0)
            weigh(0, 0)
            keep_turn(1)

            def body(g, r, u):
                for j in range(GROUP):
                    step = g * GROUP + j
                    bank, place = load_step(step)
                    hold(act, s["summed"], step + (FREE + 1), s["held_act"])
                    hold(act, s["taken"], step + (SUM_BANKS - 1), s["held_act"])
                    nc.scalar.activation(sums_of[:, bass.ds(place * width, width)], banks[:, bass.ds(bank * 512, width)],
                                         ACT.Copy).then_inc(s["taken"], 1)
                    if j == KEEP_AT and exists(g, 2):
                        keep_turn(g + 2)
                    if j == WEIGH_AT and exists(g, 1):
                        weigh(g + 1, u + 1)
            rounds(act, body)

        @block.tensor
        def _(pe):
            pe.sem_inc(s["summed"], FREE)
            pe.wait_ge(s["zeroed"], 1)
            for b in range(SUM_BANKS + 2):
                nc.tensor.matmul(banks[:, b * 512:(b + 1) * 512], zeros[:, 0:P], zeros[:, :], start=True, stop=True)

            def turn(g, u):
                pe.wait_ge(s["is_hot"], g + 1)
                if not (isinstance(g, int) and g == 0):
                    pe.wait_ge(s["turn_kept"], g)
                for j in range(GROUP):
                    ins = nc.tensor.transpose(ps_t[:, j, :], hot[:, u, j, :], k["ident"][:, :])
                ins.then_inc(s["turned"], 1)

            def load_blocks(g):
                _, blocks = nc.values_load_multi_w_load_instructions(
                    step_info[64:65, cols(g * GROUP, GROUP)], engines=(mybir.EngineType.PE,), min_val=0, max_val=BLOCKS - 1,
                    skip_runtime_bounds_check_because="the sort writes them within bounds")
                return blocks

            def source_scores(g, u, blocks):
                pe.wait_ge(s["turn_kept"], g + 1)
                if not (isinstance(g, int) and g < 2):
                    pe.wait_ge(s["added"], g - 1)
                for j in range(GROUP):
                    ins = nc.tensor.matmul(ps_s[:, u % 2, j * heads:(j + 1) * heads], hot_t[:, j, :],
                                           s_src[:, bass.ds(blocks[j] * heads, heads)], start=True, stop=True)
                ins.then_inc(s["scored"], 1)

            def load_step(step):
                _, banks_of = nc.values_load_multi_w_load_instructions(
                    step_info[0:1, cols(step * 2, 2)], engines=(mybir.EngineType.PE,), min_val=0, max_val=IDLE_BANK,
                    skip_runtime_bounds_check_because="the sort writes them within bounds")
                return banks_of

            for g in range(2):
                turn(g, g)
                source_scores(g, g, load_blocks(g))

            def body(g, r, u):
                for j in range(GROUP):
                    step = g * GROUP + j
                    bank, cleared = load_step(step)
                    pe.wait_ge(s["taken"], step + 1)
                    nc.tensor.matmul(banks[:, bass.ds(cleared * 512, 2)], zeros[:, 0:P], zeros[:, 0:2],
                                     start=True, stop=True, skip_group_check=True)
                    pe.wait_ge(s["ready"], step + 1)
                    by_source = hot[:, u, j, :] if heads > 1 else weighted_hot[:, u % 2, j, :]
                    nc.tensor.matmul(banks[:, bass.ds(bank * 512, width)], by_source, rows[:, u, j, 0:width],
                                     start=False, stop=True, skip_group_check=True).then_inc(s["summed"], 1)
                    if exists(g, 2):
                        if j == TURN_AT:
                            turn(g + 2, (u + 2) % RING)
                        if j == SCORES_AT:
                            source_scores(g + 2, u, load_blocks(g + 2))
            rounds(pe, body)


def project_out(nc, sems, k, sums1, g_heads, beta_heads, w_out, b_out, a_out, table2, s_src2):
    with ExitStack() as ctx:
        st = Stage(nc, ctx, sems, "mid")
        NORMS = CHUNK_BLOCKS * HEADS
        WIDE = CHUNK_BLOCKS * HD
        OUT = FEAT + 2
        RQ, KQ = FEAT // P, HD // P
        centred = st.sb("centred", [P, WIDE])
        normed = st.sb("normed", [P, WIDE])
        mean, spread = st.sb("mean", [P, NORMS]), st.sb("spread", [P, NORMS])
        g_row, beta_row = st.sb("g_row", [P, HD]), st.sb("beta_row", [P, HD])
        w_rows = st.sb("w_rows", [P, RQ, HD])
        w_t = st.sb("w_t", [P, KQ, OUT])
        a_cols = st.sb("a_cols", [P, RQ, 2])
        b_col = st.sb("b_col", [P, RQ])
        b_wide = st.sb("b_wide", [P, RQ, P])
        b_row = st.sb("b_row", [P, OUT])
        turned_sb = st.sb("turned_sb", [P, 2, HD])
        rows = st.sb("rows", [P, 2, ROW2])
        ps_t, ps_h = st.ps("ps_t", [P, 2, HD]), st.ps("ps_h", [P, 2, 512])
        ps_w = st.ps("ps_w", [P, 2, 512])
        names = ("w_loaded b_loaded g_loaded vec pool_seq is_centred is_squared var_ready std_ready is_normed is_affine "
                 "is_negative is_exp is_elu b_widened w_turned w_kept wa_made wa_kept turned turn_kept products rows_made")
        s = {n: st.sem(n) for n in names.split()}
        stored = [st.sem("stored0"), st.sem("stored1")]
        VEC = 5
        block = st.block()

        def both(eng, chunk):
            with eng.Fori(0, CHUNKS - 1) as c:
                chunk(c)
            chunk(CHUNKS - 1)

        def by_norm(ap):
            return ap.rearrange("p (n d) -> p n d", d=HDIM)

        def by_block(ap):
            return ap.rearrange("p (b f) -> p b f", f=HD)

        @block.sync
        def _(sp):
            sp.dma_start(w_rows[:, :, :], w_out.rearrange("(q p) f -> p q f", p=P)).then_inc(s["w_loaded"], 16)
            for side in range(2):
                part = a_out[(1 - side) * FEAT:(2 - side) * FEAT]
                sp.dma_start(a_cols[:, :, side], part.rearrange("(q p) -> p q", p=P),
                             allow_slow_non_contiguous=True).then_inc(s["w_loaded"], 16)
            sp.dma_start(b_col[:, :], b_out.rearrange("(q p) -> p q", p=P), allow_slow_non_contiguous=True)\
                .then_inc(s["b_loaded"], 16)
            sp.dma_start(b_row[:, 0:FEAT], b_out.partition_broadcast(P)).then_inc(s["b_loaded"], 16)
            sp.dma_start(g_row[:, :], g_heads.rearrange("h d -> (h d)").partition_broadcast(P)).then_inc(s["g_loaded"], 16)
            sp.dma_start(beta_row[:, :], beta_heads.rearrange("h d -> (h d)").partition_broadcast(P)).then_inc(s["g_loaded"], 16)
            for x in stored:
                sp.sem_inc(x, 16)

            def chunk(c):
                last = isinstance(c, int)
                for b in range(CHUNK_BLOCKS):
                    sp.wait_ge(s["rows_made"], c * CHUNK_BLOCKS + b + 1)
                    n = LAST if last and b == CHUNK_BLOCKS - 1 else P
                    first = c * (CHUNK_BLOCKS * P) + b * P
                    at = slice(first, first + n) if last else bass.ds(first, n)
                    sp.dma_start(table2[at, :], rows[0:n, b % 2, :]).then_inc(stored[b % 2], 16)
            both(sp, chunk)
            for half, uses in ((0, CHUNKS * 4), (1, CHUNKS * 3)):
                sp.wait_ge(stored[half], 16 * (uses + 1))

        @block.gpsimd
        def _(pool):
            pool.wait_ge(s["g_loaded"], 32)

            def chunk(c):
                pool.wait_ge(s["is_normed"], c + 1)
                nc.gpsimd.tensor_tensor(by_block(normed[:, :]), by_block(normed[:, :]), middle(g_row[:, :], CHUNK_BLOCKS),
                                        ALU.mult).then_inc(s["pool_seq"], 1)
                pool.wait_ge(s["pool_seq"], c + 1)
                nc.gpsimd.tensor_tensor(by_block(normed[:, :]), by_block(normed[:, :]), middle(beta_row[:, :], CHUNK_BLOCKS),
                                        ALU.add).then_inc(s["is_affine"], 1)
            both(pool, chunk)

        @block.vector
        def _(dve):
            nc.vector.memset(rows[:, :, :], 0.0).then_inc(s["b_widened"], 1)
            dve.wait_ge(s["b_loaded"], 32)
            nc.vector.tensor_copy(b_wide[:, :, :], column(b_col[:, :], P)).then_inc(s["b_widened"], 1)
            dve.wait_ge(s["wa_kept"], KQ + 1)

            def chunk(c):
                last = isinstance(c, int)
                seq = Chain(dve, s["vec"], c * VEC)
                off = c * WIDE
                raw = by_norm(sums1[:, off:off + WIDE] if last else sums1[:, bass.ds(off, WIDE)])
                seq.mark(nc.vector.tensor_reduce(mean[:, :], raw, AX.X, ALU.add))
                seq.wait()
                seq.mark(nc.vector.tensor_scalar(mean[:, :], mean[:, :], 1.0 / HDIM, None, ALU.mult))
                seq.wait()
                nc.vector.tensor_tensor(by_norm(centred[:, :]), raw, column(mean[:, :], HDIM), ALU.subtract)\
                    .then_inc(s["is_centred"], 1)
                dve.wait_ge(s["is_squared"], c + 1)
                nc.vector.tensor_reduce(spread[:, :], by_norm(normed[:, :]), AX.X, ALU.add).then_inc(s["var_ready"], 1)
                dve.wait_ge(s["std_ready"], c + 1)
                seq.mark(nc.vector.reciprocal(spread[:, :], spread[:, :]))
                seq.wait()
                nc.vector.tensor_tensor(by_norm(normed[:, :]), by_norm(centred[:, :]), column(spread[:, :], HDIM), ALU.mult)\
                    .then_inc(s["is_normed"], 1)
                dve.wait_ge(s["is_affine"], c + 1)
                nc.vector.tensor_scalar(centred[:, :], normed[:, :], 0.0, None, ALU.min).then_inc(s["is_negative"], 1)
                dve.wait_ge(s["is_exp"], c + 1)
                seq.mark(nc.vector.scalar_tensor_tensor(normed[:, :], normed[:, :], 0.0, centred[:, :], ALU.max, ALU.add))
                seq.wait()
                nc.vector.tensor_scalar(normed[:, :], normed[:, :], -1.0, None, ALU.add).then_inc(s["is_elu"], 1)
                for b in range(CHUNK_BLOCKS):
                    g = c * CHUNK_BLOCKS + b
                    dve.wait_ge(s["products"], g + 1)
                    dve.wait_ge(stored[b % 2], (c * (4 if b % 2 == 0 else 3) + b // 2) * 16 + 16)
                    nc.vector.tensor_tensor(rows[:, b % 2, 0:FEAT + 1], ps_h[:, b % 2, 0:FEAT + 1], b_row[:, 0:FEAT + 1], ALU.add)
                    at = slice(g, g + 1) if last else bass.ds(g, 1)
                    nc.vector.tensor_tensor(s_src2[:, at], ps_h[:, b % 2, FEAT + 1:OUT], b_row[:, FEAT + 1:OUT], ALU.add)\
                        .then_inc(s["rows_made"], 1)
                assert seq.n <= VEC
                while seq.n < VEC:
                    seq.n += 1
                    dve.sem_inc(s["vec"], 1)
            both(dve, chunk)

        @block.scalar
        def _(act):
            for q in range(KQ):
                act.wait_ge(s["w_turned"], 1)
                nc.scalar.activation(w_t[:, q, 0:FEAT], (ps_t, ps_h)[q // 2][:, q % 2, 0:FEAT], ACT.Copy).then_inc(s["w_kept"], 1)
            act.wait_ge(s["wa_made"], 1)
            for q in range(KQ):
                nc.scalar.activation(w_t[:, q, FEAT:OUT], ps_w[:, 0, 2 * q:2 * q + 2], ACT.Copy).then_inc(s["wa_kept"], 1)
            nc.scalar.activation(b_row[:, FEAT:OUT], ps_w[:, 1, 0:2], ACT.Copy).then_inc(s["wa_kept"], 1)

            def chunk(c):
                act.wait_ge(s["is_centred"], c + 1)
                nc.scalar.activation(normed[:, :], centred[:, :], ACT.Square).then_inc(s["is_squared"], 1)
                act.wait_ge(s["var_ready"], c + 1)
                nc.scalar.activation(spread[:, :], spread[:, :], ACT.Sqrt, bias=k["eps"][:, :], scale=1.0 / HDIM)\
                    .then_inc(s["std_ready"], 1)
                act.wait_ge(s["is_negative"], c + 1)
                nc.scalar.activation(centred[:, :], centred[:, :], ACT.Exp).then_inc(s["is_exp"], 1)
                for b in range(CHUNK_BLOCKS):
                    act.wait_ge(s["turned"], c * CHUNK_BLOCKS + b + 1)
                    nc.scalar.activation(turned_sb[:, b % 2, :], ps_t[:, b % 2, :], ACT.Copy).then_inc(s["turn_kept"], 1)
            both(act, chunk)

        @block.tensor
        def _(pe):
            pe.wait_ge(s["w_loaded"], 48)
            for q in range(KQ):
                for r in range(RQ):
                    ins = nc.tensor.transpose((ps_t, ps_h)[q // 2][:, q % 2, r * P:(r + 1) * P], w_rows[:, r, q * P:(q + 1) * P],
                                              k["ident"][:, :])
            ins.then_inc(s["w_turned"], 1)
            for q in range(KQ):
                for r in range(RQ):
                    nc.tensor.matmul(ps_w[:, 0, 2 * q:2 * q + 2], w_rows[:, r, q * P:(q + 1) * P], a_cols[:, r, :],
                                     start=r == 0, stop=r == RQ - 1)
            pe.wait_ge(s["b_widened"], 2)
            for r in range(RQ):
                ins = nc.tensor.matmul(ps_w[:, 1, 0:2], b_wide[:, r, :], a_cols[:, r, :], start=r == 0, stop=r == RQ - 1)
            ins.then_inc(s["wa_made"], 1)
            pe.wait_ge(s["w_kept"], KQ)
            pe.wait_ge(s["wa_kept"], KQ + 1)

            def chunk(c):
                pe.wait_ge(s["is_elu"], c + 1)

                def turn(b):
                    for q in range(KQ):
                        ins = nc.tensor.transpose(ps_t[:, b % 2, q * P:(q + 1) * P],
                                                  normed[:, b * HD + q * P:b * HD + (q + 1) * P], k["ident"][:, :])
                    ins.then_inc(s["turned"], 1)

                turn(0)
                for b in range(CHUNK_BLOCKS):
                    g = c * CHUNK_BLOCKS + b
                    pe.wait_ge(s["turn_kept"], g + 1)
                    if b >= 2:
                        pe.wait_ge(s["rows_made"], g - 1)
                    if b + 1 < CHUNK_BLOCKS:
                        turn(b + 1)
                    for q in range(KQ):
                        ins = nc.tensor.matmul(ps_h[:, b % 2, 0:OUT], turned_sb[:, b % 2, q * P:(q + 1) * P], w_t[:, q, :],
                                               start=q == 0, stop=q == KQ - 1)
                    ins.then_inc(s["products"], 1)
            both(pe, chunk)


def experts(nc, sems, k, sums2, x, g_out, beta_out, router_w, w1_sb, b1, w2_sb, b2, out):
    with ExitStack() as ctx:
        st = Stage(nc, ctx, sems, "moe")
        B = CHUNK_BLOCKS
        KQ = FEAT // P
        TOKENS = B * P
        HALF = TOKENS // 2
        WIDE = B * FEAT
        first = st.sb("first", [P, WIDE])
        work = st.sb("work", [P, WIDE])
        tokens = st.sb("tokens", [P, WIDE])
        result = st.sb("result", [P, WIDE])
        x_raw = st.sb("x_raw", [P, WIDE])
        tokens_t = st.sb("tokens_t", [P, KQ, TOKENS])
        hidden = st.sb("hidden", [P, 2, KQ, TOKENS])
        mean, spread = st.sb("mean", [P, B]), st.sb("spread", [P, B])
        g_row, beta_row = st.sb("g_row", [P, FEAT]), st.sb("beta_row", [P, FEAT])
        b1_col = st.sb("b1_col", [P, EXPERTS, KQ])
        b2_sb = st.sb("b2_sb", [EXPERTS, FEAT])
        router_rows = st.sb("router_rows", [EXPERTS, FEAT])
        router_t = st.sb("router_t", [P, KQ, EXPERTS])
        probs = st.sb("probs", [P, B, EXPERTS])
        top = st.sb("top", [P, B, EXPERTS])
        top_at = st.sb("top_at", [P, B, EXPERTS], U32)
        top_no = st.sb("top_no", [P, B, 2])
        share = st.sb("share", [P, B])
        pick = st.sb("pick", [P, 2, B, EXPERTS])
        combine = st.sb("combine", [P, B, EXPERTS])
        combine_t = st.sb("combine_t", [EXPERTS, TOKENS])
        ps_h = st.ps("ps_h", [P, 4, 512])
        ps_y = st.ps("ps_y", [P, 2, 512])
        ps_t = st.ps("ps_t", [P, 512])
        ps_l = st.ps("ps_l", [P, 512])
        names = ("loaded x_loaded b_loaded vec is_centred is_squared var_ready std_ready is_normed "
                 "is_affine pool_seq is_negative is_exp is_token turned turn_kept logits reduced is_prob combined combine_turned "
                 "combine_kept router_turned router_kept hidden_made hidden_kept sums_made sums_used finished stored held")
        s = {n: st.sem(n) for n in names.split()}
        VEC = 60
        block = st.block()

        def both(eng, chunk):
            with eng.Fori(0, CHUNKS - 1) as c:
                chunk(c)
            chunk(CHUNKS - 1)

        def by_block(ap):
            return ap.rearrange("p (b f) -> p b f", f=FEAT)

        @block.sync
        def _(sp):
            sp.dma_start(router_rows[:, :], router_w).then_inc(s["loaded"], 16)
            sp.dma_start(g_row[:, :], g_out.partition_broadcast(P)).then_inc(s["loaded"], 16)
            sp.dma_start(beta_row[:, :], beta_out.partition_broadcast(P)).then_inc(s["loaded"], 16)
            sp.dma_start(b2_sb[:, :], b2).then_inc(s["b_loaded"], 16)
            for q in range(KQ):
                sp.dma_start(b1_col[:, :, q], b1[:, q * P:(q + 1) * P].rearrange("e p -> p e"),
                             allow_slow_non_contiguous=True).then_inc(s["b_loaded"], 16)

            with sp.Fori(0, CHUNKS - 1) as c:
                sp.wait_ge(s["finished"], c + 1)
                sp.dma_start(out[bass.ds(c * TOKENS, TOKENS), :].rearrange("(b p) f -> p b f", p=P),
                             by_block(result[:, :])).then_inc(s["stored"], 16)
            c = CHUNKS - 1
            sp.wait_ge(s["finished"], c + 1)
            full = (B - 1) * P
            sp.dma_start(out[c * TOKENS:c * TOKENS + full, :].rearrange("(b p) f -> p b f", p=P),
                         by_block(result[:, :])[:, 0:B - 1, :]).then_inc(s["stored"], 16)
            sp.dma_start(out[c * TOKENS + full:NODES, :], by_block(result[:, :])[0:LAST, B - 1, :]).then_inc(s["stored"], 16)
            sp.wait_ge(s["stored"], 16 * (CHUNKS + 2))

        @block.gpsimd
        def _(pool):
            def load(c, rows_of_last):
                at, full = c * TOKENS, (B - 1) * P
                static = isinstance(c, int)
                most = x[at:at + full, :] if static else x[bass.ds(at, full), :]
                rest = x[at + full:at + full + rows_of_last, :] if static else x[bass.ds(at + full, rows_of_last), :]
                nc.gpsimd.dma_start(by_block(x_raw[:, :])[:, 0:B - 1, :], most.rearrange("(b p) f -> p b f", p=P))\
                    .then_inc(s["x_loaded"], 16)
                nc.gpsimd.dma_start(by_block(x_raw[:, :])[0:rows_of_last, B - 1, :], rest).then_inc(s["x_loaded"], 16)

            load(0, P)
            pool.wait_ge(s["loaded"], 48)

            def affine(c):
                pool.wait_ge(s["is_normed"], c * 2 + 1)
                nc.gpsimd.tensor_tensor(by_block(tokens[:, :]), by_block(tokens[:, :]), middle(g_row[:, :], B), ALU.mult)\
                    .then_inc(s["pool_seq"], 1)
                pool.wait_ge(s["pool_seq"], c + 1)
                nc.gpsimd.tensor_tensor(by_block(tokens[:, :]), by_block(tokens[:, :]), middle(beta_row[:, :], B), ALU.add)\
                    .then_inc(s["is_affine"], 1)

            with pool.Fori(0, CHUNKS - 2) as c:
                affine(c)
                hold(pool, s["is_centred"], c * 2 + 2, s["held"])
                load(c + 1, P)
            affine(CHUNKS - 2)
            pool.wait_ge(s["is_centred"], 2 * (CHUNKS - 1))
            load(CHUNKS - 1, LAST)
            affine(CHUNKS - 1)

        @block.vector
        def _(dve):
            def normalise(seq, raw, c, turn):
                seq.mark(nc.vector.tensor_reduce(mean[:, :], raw, AX.X, ALU.add))
                seq.wait()
                seq.mark(nc.vector.tensor_scalar(mean[:, :], mean[:, :], 1.0 / FEAT, None, ALU.mult))
                seq.wait()
                nc.vector.tensor_tensor(by_block(work[:, :]), raw, column(mean[:, :], FEAT), ALU.subtract)\
                    .then_inc(s["is_centred"], 1)
                dve.wait_ge(s["is_squared"], c * 2 + turn)
                nc.vector.tensor_reduce(spread[:, :], by_block(tokens[:, :]), AX.X, ALU.add).then_inc(s["var_ready"], 1)
                dve.wait_ge(s["std_ready"], c * 2 + turn)
                seq.mark(nc.vector.reciprocal(spread[:, :], spread[:, :]))
                seq.wait()
                nc.vector.tensor_tensor(by_block(tokens[:, :]), by_block(work[:, :]), column(spread[:, :], FEAT), ALU.mult)\
                    .then_inc(s["is_normed"], 1)

            def chunk(c):
                last = isinstance(c, int)
                seq = Chain(dve, s["vec"], c * VEC)
                off = c * WIDE
                raw = by_block(sums2[:, off:off + WIDE] if last else sums2[:, bass.ds(off, WIDE)])
                normalise(seq, raw, c, 1)
                dve.wait_ge(s["is_affine"], c + 1)
                nc.vector.tensor_scalar(work[:, :], tokens[:, :], 0.0, None, ALU.min).then_inc(s["is_negative"], 1)
                dve.wait_ge(s["is_exp"], c + 1)
                seq.mark(nc.vector.scalar_tensor_tensor(first[:, :], tokens[:, :], 0.0, work[:, :], ALU.max, ALU.add))
                seq.wait()
                dve.wait_ge(s["x_loaded"], c * 32 + 32)
                seq.mark(nc.vector.scalar_tensor_tensor(first[:, :], first[:, :], -1.0, x_raw[:, :], ALU.add, ALU.add))
                seq.wait()
                normalise(seq, by_block(first[:, :]), c, 2)
                dve.wait_ge(s["logits"], c + 1)
                l3 = ps_l[:, 0:B * EXPERTS].rearrange("p (b e) -> p b e", e=EXPERTS)
                seq.mark(nc.vector.tensor_reduce(share[:, :], l3, AX.X, ALU.max))
                seq.wait()
                nc.vector.tensor_tensor(probs[:, :, :], l3, column(share[:, :], EXPERTS), ALU.subtract).then_inc(s["reduced"], 1)
                dve.wait_ge(s["is_prob"], c + 1)
                seq.mark(nc.vector.tensor_reduce(share[:, :], probs[:, :, :], AX.X, ALU.add))
                seq.wait()
                seq.mark(nc.vector.reciprocal(share[:, :], share[:, :]))
                seq.wait()
                seq.mark(nc.vector.tensor_tensor(probs[:, :, :], probs[:, :, :], column(share[:, :], EXPERTS), ALU.mult))
                hold(dve, s["vec"], seq.base + seq.n, s["held"])
                for b in range(B):
                    seq.mark(nc.vector.max(top[:, b, :], probs[:, b, :]))
                hold(dve, s["vec"], seq.base + seq.n, s["held"])
                for b in range(B):
                    seq.mark(nc.vector.max_index(top_at[:, b, :], top[:, b, :], probs[:, b, :]))
                seq.wait()
                seq.mark(nc.vector.tensor_copy(top_no[:, :, :], top_at[:, :, 0:2]))
                seq.mark(nc.vector.tensor_tensor(share[:, :], top[:, :, 0], top[:, :, 1], ALU.add))
                seq.wait()
                seq.mark(nc.vector.tensor_scalar(share[:, :], share[:, :], 1e-12, None, ALU.max))
                seq.wait()
                seq.mark(nc.vector.reciprocal(share[:, :], share[:, :]))
                for n in range(2):
                    seq.mark(nc.vector.tensor_tensor(pick[:, n, :, :], middle(k["iota"][:, 0:EXPERTS], B),
                                                     column(top_no[:, :, n], EXPERTS), ALU.is_equal))
                seq.wait()
                for n in range(2):
                    seq.mark(nc.vector.tensor_tensor(pick[:, n, :, :], pick[:, n, :, :], column(top[:, :, n], EXPERTS), ALU.mult))
                seq.wait()
                seq.mark(nc.vector.tensor_tensor(combine[:, :, :], pick[:, 0, :, :], pick[:, 1, :, :], ALU.add))
                seq.wait()
                nc.vector.tensor_tensor(combine[:, :, :], combine[:, :, :], column(share[:, :], EXPERTS), ALU.mult)\
                    .then_inc(s["combined"], 1)
                dve.wait_ge(s["stored"], c * 16 + 16)
                seq.mark(nc.vector.tensor_tensor(result[:, :], first[:, :], tokens[:, :], ALU.add))
                seq.wait()
                for e in range(-1, EXPERTS):
                    for b in range(B):
                        n = (e + 1) * B + b
                        dve.wait_ge(s["sums_made"], c * ((EXPERTS + 1) * B) + (n + 1))
                        here = result[:, b * FEAT:(b + 1) * FEAT]
                        if e < 0:
                            ins = nc.vector.tensor_tensor(here, ps_y[:, n % 2, 0:FEAT], here, ALU.add)
                        else:
                            if b == 0:
                                dve.wait_ge(s["sums_used"], c * ((EXPERTS + 1) * B) + n)
                            ins = nc.vector.scalar_tensor_tensor(here, ps_y[:, n % 2, 0:FEAT], combine[:, b, e:e + 1], here,
                                                                 ALU.mult, ALU.add)
                        ins.then_inc(s["sums_used"], 1)
                dve.wait_ge(s["sums_used"], (c + 1) * ((EXPERTS + 1) * B))
                dve.sem_inc(s["finished"], 1)
                assert seq.n <= VEC
                dve.sem_inc(s["vec"], VEC - seq.n)
            dve.sem_inc(s["stored"], 16)
            both(dve, chunk)

        @block.scalar
        def _(act):
            act.wait_ge(s["router_turned"], 1)
            nc.scalar.activation(router_t[:, :, :], ps_t[:, 0:KQ * EXPERTS].rearrange("p (q e) -> p q e", q=KQ), ACT.Copy)\
                .then_inc(s["router_kept"], 1)
            act.wait_ge(s["b_loaded"], 48)

            def chunk(c):
                def spread_of(turn):
                    act.wait_ge(s["is_centred"], c * 2 + turn)
                    nc.scalar.activation(tokens[:, :], work[:, :], ACT.Square).then_inc(s["is_squared"], 1)
                    act.wait_ge(s["var_ready"], c * 2 + turn)
                    nc.scalar.activation(spread[:, :], spread[:, :], ACT.Sqrt, bias=k["eps"][:, :], scale=1.0 / FEAT)\
                        .then_inc(s["std_ready"], 1)
                spread_of(1)
                act.wait_ge(s["is_negative"], c + 1)
                nc.scalar.activation(work[:, :], work[:, :], ACT.Exp).then_inc(s["is_exp"], 1)
                spread_of(2)
                for q in range(KQ * 2):
                    act.wait_ge(s["turned"], c * (KQ * 2) + (q + 1))
                    half, kq = q // KQ, q % KQ
                    span = 4 if half == 0 else B - 4
                    nc.scalar.activation(tokens_t[:, kq, half * 4 * P:(half * 4 + span) * P], ps_h[:, q, 0:span * P], ACT.Copy)\
                        .then_inc(s["turn_kept"], 1)
                act.wait_ge(s["reduced"], c + 1)
                nc.scalar.activation(probs[:, :, :], probs[:, :, :], ACT.Exp).then_inc(s["is_prob"], 1)
                act.wait_ge(s["combine_turned"], c * 2 + 1)
                nc.scalar.activation(combine_t[:, 0:4 * P], ps_t[0:EXPERTS, :], ACT.Copy).then_inc(s["combine_kept"], 1)
                act.wait_ge(s["combine_turned"], c * 2 + 2)
                nc.scalar.activation(combine_t[:, 4 * P:TOKENS], ps_t[0:EXPERTS, 0:TOKENS - 4 * P], ACT.Copy)\
                    .then_inc(s["combine_kept"], 1)
                for e in range(EXPERTS):
                    for n in range(4):
                        half, unit = n // 2, n % 2
                        act.wait_ge(s["hidden_made"], c * (4 * EXPERTS) + (4 * e + n + 1))
                        if e >= 2 and n == 0:
                            act.wait_ge(s["sums_made"], c * ((EXPERTS + 1) * B) + e * B)
                        nc.scalar.activation(hidden[:, e % 2, unit, half * HALF:(half + 1) * HALF], ps_h[:, n, 0:HALF], ACT.Gelu,
                                             bias=b1_col[:, e, unit:unit + 1]).then_inc(s["hidden_kept"], 1)
            both(act, chunk)

        @block.tensor
        def _(pe):
            pe.wait_ge(s["loaded"], 48)
            for q in range(KQ):
                ins = nc.tensor.transpose(ps_t[:, q * EXPERTS:(q + 1) * EXPERTS], router_rows[:, q * P:(q + 1) * P],
                                          k["ident"][0:EXPERTS, 0:EXPERTS])
            ins.then_inc(s["router_turned"], 1)
            pe.wait_ge(s["router_kept"], 1)
            pe.wait_ge(s["b_loaded"], 48)

            def chunk(c):
                pe.wait_ge(s["is_normed"], c * 2 + 2)
                for q in range(KQ * 2):
                    half, kq = q // KQ, q % KQ
                    for b in range(4 if half == 0 else B - 4):
                        at = (half * 4 + b) * FEAT + kq * P
                        ins = nc.tensor.transpose(ps_h[:, q, b * P:(b + 1) * P], tokens[:, at:at + P], k["ident"][:, :])
                    ins.then_inc(s["turned"], 1)
                pe.wait_ge(s["turn_kept"], c * (KQ * 2) + KQ * 2)
                for b in range(B):
                    for kq in range(KQ):
                        ins = nc.tensor.matmul(ps_l[:, b * EXPERTS:(b + 1) * EXPERTS], tokens_t[:, kq, b * P:(b + 1) * P],
                                               router_t[:, kq, :], start=kq == 0, stop=kq == KQ - 1)
                ins.then_inc(s["logits"], 1)

                def hidden_of(e):
                    for n in range(4):
                        half, unit = n // 2, n % 2
                        if e:
                            pe.wait_ge(s["hidden_kept"], c * (4 * EXPERTS) + (4 * (e - 1) + n + 1))
                        for kq in range(KQ):
                            ins = nc.tensor.matmul(ps_h[:, n, 0:HALF], w1_sb[:, kq, e, unit * P:(unit + 1) * P],
                                                   tokens_t[:, kq, half * HALF:(half + 1) * HALF],
                                                   start=kq == 0, stop=kq == KQ - 1)
                        ins.then_inc(s["hidden_made"], 1)

                hidden_of(0)
                pe.wait_ge(s["combined"], c + 1)
                for half in range(2):
                    if half:
                        pe.wait_ge(s["combine_kept"], c * 2 + 1)
                    for b in range(4 if half == 0 else B - 4):
                        ins = nc.tensor.transpose(ps_t[0:EXPERTS, b * P:(b + 1) * P], combine[:, half * 4 + b, :], k["ident"][:, :])
                    ins.then_inc(s["combine_turned"], 1)
                pe.wait_ge(s["combine_kept"], c * 2 + 2)

                def free_bank(n):
                    if n >= 2:
                        pe.wait_ge(s["sums_used"], c * ((EXPERTS + 1) * B) + (n - 1))
                for b in range(B):
                    free_bank(b)
                    nc.tensor.matmul(ps_y[:, b % 2, 0:FEAT], combine_t[:, b * P:(b + 1) * P], b2_sb[:, :], start=True, stop=True)\
                        .then_inc(s["sums_made"], 1)
                for e in range(EXPERTS):
                    if e + 1 < EXPERTS:
                        hidden_of(e + 1)
                    pe.wait_ge(s["hidden_kept"], c * (4 * EXPERTS) + 4 * (e + 1))
                    for b in range(B):
                        n = (e + 1) * B + b
                        free_bank(n)
                        for unit in range(KQ):
                            ins = nc.tensor.matmul(ps_y[:, n % 2, 0:FEAT], hidden[:, e % 2, unit, b * P:(b + 1) * P],
                                                   w2_sb[:, unit, e, :], start=unit == 0, stop=unit == KQ - 1)
                        ins.then_inc(s["sums_made"], 1)
            both(pe, chunk)


def build(nc, t):
    with ExitStack() as ctx, ExitStack() as sems:
        k = constants(nc, ctx, sems)
        shared = Stage(nc, ctx, sems, "shared")
        s_src1 = shared.sb("s_src1", [P, BLOCKS, HEADS])
        node_of = shared.sb("node_of", [P, STEPS], I32)
        local_of = shared.sb("local_of", [P, STEPS])
        step_info = shared.sb("step_info", [P, STEPS * 2], I32)
        s_src2 = shared.sb("s_src2", [P, BLOCKS])
        table1 = nc.dram_tensor("table1", [NODES, ROW1], FP32, kind="Internal").ap()
        table2 = nc.dram_tensor("table2", [NODES, ROW2], FP32, kind="Internal").ap()
        gnn = {n: t["L0_gnn_" + n] for n in ("W_heads b_heads a_heads g_heads beta_heads W_out b_out a_out g_out beta_out").split()}
        ffn = {n: t["L0_ffn_" + n] for n in "router_w w1 b1 w2 b2".split()}

        project_heads(nc, sems, k, t["x"], gnn["W_heads"], gnn["b_heads"], gnn["a_heads"], table1, s_src1)
        sort_edges(nc, sems, k, t["src"], t["dst"], node_of, local_of, step_info)
        with ExitStack() as heads:
            sums1 = heads.enter_context(nc.sbuf_tensor("sums1", [P, (BLOCKS + 2) * HD], FP32))
            aggregate(nc, sems, k, "heads", table1, ROW1, HD, HEADS, s_src1[:, :, :].rearrange("p b h -> p (b h)"),
                      node_of, local_of, step_info, sums1)
            project_out(nc, sems, k, sums1, gnn["g_heads"], gnn["beta_heads"], gnn["W_out"], gnn["b_out"], gnn["a_out"],
                        table2, s_src2)
        late = Stage(nc, ctx, sems, "late")
        sums2 = late.sb("sums2", [P, (BLOCKS + 2) * FEAT])
        w1_sb = late.sb("w1", [P, FEAT // P, EXPERTS, FEAT])
        w2_sb = late.sb("w2", [P, FEAT // P, EXPERTS, FEAT])
        loads = [(sb[:, q, :, :], w[:, q * P:(q + 1) * P, :].rearrange("e p f -> p e f"))
                 for sb, w in ((w1_sb, ffn["w1"]), (w2_sb, ffn["w2"])) for q in range(FEAT // P)]
        aggregate(nc, sems, k, "out", table2, ROW2, FEAT, 1, s_src2, node_of, local_of, step_info, sums2, loads)
        experts(nc, sems, k, sums2, t["x"], gnn["g_out"], gnn["beta_out"], ffn["router_w"], w1_sb, ffn["b1"], w2_sb,
                ffn["b2"], t["out"])


def kernel(**inputs):
    import numpy as np
    import concourse.bacc as bacc
    from concourse.bass_utils import run_bass_kernel_spmd as run

    nc = bacc.Bacc("TRN2", target_bir_lowering=False, num_devices=1)
    arrays, tensors = {}, {}
    for name, value in inputs.items():
        arrays[f"in_{name}"] = a = np.ascontiguousarray(value)
        tensors[name] = nc.dram_tensor(f"in_{name}", a.shape, mybir.dt.from_np(a.dtype), kind="ExternalInput").ap()
    tensors["out"] = nc.dram_tensor("out", (NODES, FEAT), FP32, kind="ExternalOutput").ap()
    build(nc, tensors)
    return run(nc, [arrays], core_ids=[0]).results[0]["out"]
```

```python
import concourse.bass as bass
from concourse import mybir
from contextlib import ExitStack

FP32 = mybir.dt.float32
BF16 = mybir.dt.bfloat16
FP16 = mybir.dt.float16
I32 = mybir.dt.int32
U16 = mybir.dt.uint16
U32 = mybir.dt.uint32
ALU = mybir.AluOpType
ACT = mybir.ActivationFunctionType
AX = mybir.AxisListType

P = 128
NODES = 6250
FEAT = 256
HEADS = 8
HDIM = 64
HD = HEADS * HDIM
EDGES = 206250
EXPERTS = 8
LN_EPS = 1e-5
SLOPE = 0.2

BLOCKS = -(-NODES // P)
LAST = NODES - (BLOCKS - 1) * P
CHUNK_BLOCKS = 7
CHUNKS = BLOCKS // CHUNK_BLOCKS
assert CHUNKS * CHUNK_BLOCKS == BLOCKS

EP = max(p for p in range(1, P + 1) if EDGES % p == 0)
ECOLS = EDGES // EP
PARTS = 6
PCOLS = ECOLS // PARTS
assert PARTS * PCOLS == ECOLS
PART_TILES = (EP * PCOLS + 2 * (P - 1) * BLOCKS) // P
GROUP = 4
RING = 6
STEPS = -(-((EDGES + P * BLOCKS) // P) // GROUP) * GROUP
GROUPS = STEPS // GROUP
ROUNDS = (GROUPS - GROUP) // RING
DST_LOW = 1024
MAGIC = 1.5 * 2.0 ** 23
NOWHERES = 4
SUM_BANKS = 3
IDLE_BANK, SPARE_BANK = 3, 4
NOWHERE = 100000.0
NO_NODE = 1000.0

ROW1 = HD + HEADS
ROW2 = FEAT + 4


class Chain:

    def __init__(self, eng, sem, base=0):
        self.eng, self.sem, self.base, self.n = eng, sem, base, 0

    def mark(self, ins):
        ins.then_inc(self.sem, 1)
        self.n += 1

    def wait(self):
        self.eng.wait_ge(self.sem, self.base + self.n)


def hold(eng, sem, value, scratch):
    eng.wait_ge(sem, value)
    eng.sem_inc(scratch, 1)


def column(ap, width):
    return ap.unsqueeze(2).to_broadcast([ap.shape[0], ap.shape[1], width])


def middle(ap, count):
    return ap.unsqueeze(1).to_broadcast([ap.shape[0], count, ap.shape[1]])


class Stage:

    def __init__(self, nc, ctx, sems, name):
        self.nc, self.ctx, self.sems, self.name = nc, ctx, sems, name

    def sb(self, name, shape, dt=FP32):
        return self.ctx.enter_context(self.nc.sbuf_tensor(f"{self.name}_{name}", shape, dt))

    def ps(self, name, shape, dt=FP32):
        return self.ctx.enter_context(self.nc.psum_tensor(f"{self.name}_{name}", shape, dt))

    def sem(self, name):
        return self.sems.enter_context(self.nc.semaphore(f"{self.name}_{name}"))

    def block(self):
        return self.ctx.enter_context(self.nc.Block())


def constants(nc, ctx, sems):
    st = Stage(nc, ctx, sems, "const")
    k = {
        "ident": st.sb("ident", [P, P]),
        "iota": st.sb("iota", [P, P]),
        "iota_p": st.sb("iota_p", [P, 1]),
        "eps": st.sb("eps", [P, 1]),
    }
    zeroed, counted = st.sem("zeroed"), st.sem("counted")
    with ExitStack() as inner:
        block = inner.enter_context(nc.Block())

        @block.gpsimd
        def _(pool):
            nc.gpsimd.memset(k["ident"][:, :], 0.0).then_inc(zeroed, 1)
            nc.gpsimd.memset(k["eps"][:, :], LN_EPS)
            nc.gpsimd.iota(k["iota"][:, :], pattern=[[1, P]], base=0, channel_multiplier=0,
                           allow_small_or_imprecise_dtypes=True)
            nc.gpsimd.iota(k["iota_p"][:, :], pattern=[[0, 1]], base=0, channel_multiplier=1,
                           allow_small_or_imprecise_dtypes=True)
            pool.wait_ge(zeroed, 1)
            nc.gpsimd.affine_select(out=k["ident"][:, :], in_=k["ident"][:, :], compare_op=ALU.not_equal,
                                    fill=1.0, base=0, pattern=[[-1, P]], channel_multiplier=1).then_inc(counted, 1)
    return k


def project_heads(nc, sems, k, x, w_heads, b_heads, a_heads, table1, s_src1):
    with ExitStack() as ctx:
        st = Stage(nc, ctx, sems, "proj")
        x_raw = st.sb("x_raw", [P, CHUNK_BLOCKS, FEAT])
        centred = st.sb("centred", [P, CHUNK_BLOCKS, FEAT])
        squares = st.sb("squares", [P, CHUNK_BLOCKS, FEAT])
        normed = st.sb("normed", [P, CHUNK_BLOCKS, FEAT])
        mean = st.sb("mean", [P, CHUNK_BLOCKS])
        spread = st.sb("spread", [P, CHUNK_BLOCKS])
        w_rows = st.sb("w_rows", [P, HD // P, FEAT])
        w_t = st.sb("w_t", [P, FEAT // P, HD])
        a_cols = st.sb("a_cols", [P, HD // P, 2 * HEADS])
        wa = st.sb("wa", [P, FEAT // P, 2 * HEADS])
        b_col = st.sb("b_col", [P, HD // P])
        b_wide = st.sb("b_wide", [P, HD // P, P])
        b_row = st.sb("b_row", [P, HD])
        ba_row = st.sb("ba_row", [P, 2 * HEADS])
        normed_t = st.sb("normed_t", [P, 2, FEAT])
        rows = st.sb("rows", [P, 2, ROW1])
        ps_t = st.ps("ps_t", [P, 2, 512])
        ps_h = st.ps("ps_h", [P, 2, 512])
        ps_s = st.ps("ps_s", [P, 2, 512])

        w_loaded, b_loaded, a_zeroed, a_loaded = (st.sem(n) for n in ("w_loaded", "b_loaded", "a_zeroed", "a_loaded"))
        x_loaded, vec, is_centred, is_squared, std_ready = (
            st.sem(n) for n in ("x_loaded", "vec", "is_centred", "is_squared", "std_ready"))
        var_ready, is_normed, b_widened = st.sem("var_ready"), st.sem("is_normed"), st.sem("b_widened")
        w_turned, w_kept, wa_made, wa_kept = (st.sem(n) for n in ("w_turned", "w_kept", "wa_made", "wa_kept"))
        turned, turn_kept, products, rows_made = (st.sem(n) for n in ("turned", "turn_kept", "products", "rows_made"))
        pool_held = st.sem("pool_held")
        stored = [st.sem("stored0"), st.sem("stored1")]
        VEC = 3
        block = st.block()

        def both(eng, chunk):
            with eng.Fori(0, CHUNKS - 1) as c:
                chunk(c)
            chunk(CHUNKS - 1)

        @block.sync
        def _(sp):
            flat_w = w_heads.rearrange("h d f -> (h d) f").rearrange("(q p) f -> p q f", p=P)
            flat_b = b_heads.rearrange("h d -> (h d)")
            sp.dma_start(w_rows[:, :, :], flat_w).then_inc(w_loaded, 16)
            sp.dma_start(b_col[:, :], flat_b.rearrange("(q p) -> p q", p=P),
                         allow_slow_non_contiguous=True).then_inc(b_loaded, 16)
            sp.dma_start(b_row[:, :], flat_b.partition_broadcast(P)).then_inc(b_loaded, 16)
            sp.wait_ge(a_zeroed, 1)
            for h in range(HEADS):
                at = slice(h % 2 * HDIM, h % 2 * HDIM + HDIM)
                for side in range(2):
                    column_of = side * HEADS + h
                    sp.dma_start(a_cols[at, h // 2, column_of:column_of + 1],
                                 a_heads[h, side * HDIM:(side + 1) * HDIM].unsqueeze(1),
                                 allow_slow_non_contiguous=True).then_inc(a_loaded, 16)
            for s in stored:
                sp.sem_inc(s, 16)

            def chunk(c):
                last = isinstance(c, int)
                for b in range(CHUNK_BLOCKS):
                    sp.wait_ge(rows_made, c * CHUNK_BLOCKS + b + 1)
                    n = LAST if last and b == CHUNK_BLOCKS - 1 else P
                    first = c * (CHUNK_BLOCKS * P) + b * P
                    at = slice(first, first + n) if last else bass.ds(first, n)
                    sp.dma_start(table1[at, :], rows[0:n, b % 2, :]).then_inc(stored[b % 2], 16)
            both(sp, chunk)
            for half, uses in ((0, CHUNKS * 4), (1, CHUNKS * 3)):
                sp.wait_ge(stored[half], 16 * (uses + 1))

        @block.gpsimd
        def _(pool):
            nc.gpsimd.dma_start(x_raw[:, :, :], x[0:CHUNK_BLOCKS * P, :]
                                .rearrange("(b p) f -> p b f", p=P)).then_inc(x_loaded, 16)
            nc.gpsimd.memset(a_cols[:, :, :], 0.0).then_inc(a_zeroed, 1)
            with pool.Fori(0, CHUNKS - 2) as c:
                hold(pool, is_centred, c + 1, pool_held)
                nc.gpsimd.dma_start(x_raw[:, :, :], x[bass.ds((c + 1) * (CHUNK_BLOCKS * P), CHUNK_BLOCKS * P), :]
                                    .rearrange("(b p) f -> p b f", p=P)).then_inc(x_loaded, 16)
            pool.wait_ge(is_centred, CHUNKS - 1)
            tail = (CHUNKS - 1) * CHUNK_BLOCKS * P
            full = (CHUNK_BLOCKS - 1) * P
            nc.gpsimd.dma_start(x_raw[:, 0:CHUNK_BLOCKS - 1, :],
                                x[tail:tail + full, :].rearrange("(b p) f -> p b f", p=P)).then_inc(x_loaded, 16)
            nc.gpsimd.dma_start(x_raw[0:LAST, CHUNK_BLOCKS - 1, :], x[tail + full:NODES, :]).then_inc(x_loaded, 16)

        @block.vector
        def _(dve):
            dve.wait_ge(b_loaded, 32)
            nc.vector.tensor_copy(b_wide[:, :, :], column(b_col[:, :], P)).then_inc(b_widened, 1)
            dve.wait_ge(wa_kept, 1)

            def chunk(c):
                last = isinstance(c, int)
                seq = Chain(dve, vec, c * VEC)
                dve.wait_ge(x_loaded, 16 * (CHUNKS + 1) if last else c * 16 + 16)
                seq.mark(nc.vector.tensor_reduce(mean[:, :], x_raw[:, :, :], AX.X, ALU.add))
                seq.wait()
                seq.mark(nc.vector.tensor_scalar(mean[:, :], mean[:, :], 1.0 / FEAT, None, ALU.mult))
                seq.wait()
                nc.vector.tensor_tensor(centred[:, :, :], x_raw[:, :, :], column(mean[:, :], FEAT),
                                        ALU.subtract).then_inc(is_centred, 1)
                dve.wait_ge(is_squared, c + 1)
                nc.vector.tensor_reduce(spread[:, :], squares[:, :, :], AX.X, ALU.add).then_inc(var_ready, 1)
                dve.wait_ge(std_ready, c + 1)
                seq.mark(nc.vector.reciprocal(spread[:, :], spread[:, :]))
                seq.wait()
                nc.vector.tensor_tensor(normed[:, :, :], centred[:, :, :], column(spread[:, :], FEAT),
                                        ALU.mult).then_inc(is_normed, 1)
                for b in range(CHUNK_BLOCKS):
                    g = c * CHUNK_BLOCKS + b
                    dve.wait_ge(products, g + 1)
                    use = c * (4 if b % 2 == 0 else 3) + b // 2
                    dve.wait_ge(stored[b % 2], use * 16 + 16)
                    nc.vector.tensor_tensor(rows[:, b % 2, 0:HD], ps_h[:, b % 2, :], b_row[:, :], ALU.add)
                    nc.vector.tensor_tensor(rows[:, b % 2, HD:ROW1], ps_s[:, b % 2, HEADS:2 * HEADS],
                                            ba_row[:, HEADS:2 * HEADS], ALU.add)
                    at = g if last else bass.ds(g, 1)
                    out = s_src1[:, at, :] if last else s_src1[:, at, :].rearrange("p o h -> p (o h)")
                    nc.vector.tensor_tensor(out, ps_s[:, b % 2, 0:HEADS], ba_row[:, 0:HEADS],
                                            ALU.add).then_inc(rows_made, 1)
                assert seq.n == VEC
            both(dve, chunk)

        @block.scalar
        def _(act):
            act.wait_ge(w_turned, 1)
            for f in range(FEAT // P):
                nc.scalar.activation(w_t[:, f, :], ps_h[:, f, :], ACT.Copy).then_inc(w_kept, 1)
            act.wait_ge(wa_made, 1)
            for f in range(FEAT // P):
                nc.scalar.activation(wa[:, f, :], ps_s[:, f, 0:2 * HEADS], ACT.Copy)
            nc.scalar.activation(ba_row[:, :], ps_t[:, 0, 0:2 * HEADS], ACT.Copy).then_inc(wa_kept, 1)

            def chunk(c):
                act.wait_ge(is_centred, c + 1)
                nc.scalar.activation(squares[:, :, :], centred[:, :, :], ACT.Square).then_inc(is_squared, 1)
                act.wait_ge(var_ready, c + 1)
                nc.scalar.activation(spread[:, :], spread[:, :], ACT.Sqrt, bias=k["eps"][:, :],
                                     scale=1.0 / FEAT).then_inc(std_ready, 1)
                for b in range(CHUNK_BLOCKS):
                    g = c * CHUNK_BLOCKS + b
                    act.wait_ge(turned, g + 1)
                    nc.scalar.activation(normed_t[:, b % 2, :], ps_t[:, b % 2, 0:FEAT], ACT.Copy).then_inc(turn_kept, 1)
            both(act, chunk)

        @block.tensor
        def _(pe):
            pe.wait_ge(w_loaded, 16)
            for f in range(FEAT // P):
                for q in range(HD // P):
                    ins = nc.tensor.transpose(ps_h[:, f, q * P:(q + 1) * P], w_rows[:, q, f * P:(f + 1) * P], k["ident"][:, :])
            ins.then_inc(w_turned, 1)
            pe.wait_ge(a_loaded, 16 * 2 * HEADS)
            for f in range(FEAT // P):
                for q in range(HD // P):
                    nc.tensor.matmul(ps_s[:, f, 0:2 * HEADS], w_rows[:, q, f * P:(f + 1) * P], a_cols[:, q, :],
                                     start=q == 0, stop=q == HD // P - 1)
            pe.wait_ge(b_widened, 1)
            for q in range(HD // P):
                ins = nc.tensor.matmul(ps_t[:, 0, 0:2 * HEADS], b_wide[:, q, :], a_cols[:, q, :],
                                       start=q == 0, stop=q == HD // P - 1)
            ins.then_inc(wa_made, 1)
            pe.wait_ge(w_kept, FEAT // P)
            pe.wait_ge(wa_kept, 1)

            def chunk(c):
                pe.wait_ge(is_normed, c + 1)

                def turn(b):
                    for f in range(FEAT // P):
                        ins = nc.tensor.transpose(ps_t[:, b % 2, f * P:(f + 1) * P], normed[:, b, f * P:(f + 1) * P],
                                                  k["ident"][:, :])
                    ins.then_inc(turned, 1)

                turn(0)
                for b in range(CHUNK_BLOCKS):
                    g = c * CHUNK_BLOCKS + b
                    pe.wait_ge(turn_kept, g + 1)
                    if b >= 2:
                        pe.wait_ge(rows_made, g - 1)
                    if b + 1 < CHUNK_BLOCKS:
                        turn(b + 1)
                    for f in range(FEAT // P):
                        nc.tensor.matmul(ps_h[:, b % 2, :], normed_t[:, b % 2, f * P:(f + 1) * P], w_t[:, f, :],
                                         start=f == 0, stop=f == FEAT // P - 1)
                    for f in range(FEAT // P):
                        ins = nc.tensor.matmul(ps_s[:, b % 2, 0:2 * HEADS], normed_t[:, b % 2, f * P:(f + 1) * P],
                                               wa[:, f, :], start=f == 0, stop=f == FEAT // P - 1)
                    ins.then_inc(products, 1)
            both(pe, chunk)


def sort_edges(nc, sems, k, src, dst, node_of, local_of, step_info):
    with ExitStack() as ctx:
        st = Stage(nc, ctx, sems, "sort")
        RANKS = 4
        UNROLL = 12
        assert BLOCKS % UNROLL == 1 and UNROLL % RANKS == 0
        src_i, dst_i = st.sb("src_i", [EP, ECOLS], I32), st.sb("dst_i", [EP, ECOLS], I32)
        scratch_i = st.sb("scratch_i", [EP, ECOLS], I32)
        key = st.sb("key", [EP, ECOLS], BF16)
        low, high = st.sb("low", [EP, ECOLS]), st.sb("high", [EP, ECOLS])
        place = st.sb("place", [EP, PARTS, PCOLS])
        lane, tile = (src_i[:, n * PCOLS:(n + 1) * PCOLS].bitcast(FP32) for n in range(2))
        place_i = src_i[:, 2 * PCOLS:3 * PCOLS]
        member_all = st.sb("member", [P, max(BLOCKS * PCOLS, 14 * STEPS)], BF16)
        member = member_all[0:EP, 0:BLOCKS * PCOLS]
        mask = st.sb("mask", [EP, RANKS, PCOLS], U16)
        before = st.sb("before", [P, P])
        before_b = st.sb("before_b", [EP, P], BF16)
        step_back = st.sb("step_back", [P, P])
        one_column = st.sb("one_column", [EP, 2 * P], BF16)
        row_of = st.sb("row_of", [P, BLOCKS, P], BF16)
        zeros_b = st.sb("zeros_b", [P, PCOLS], BF16)
        zeros_h = st.sb("zeros_h", [EP, PART_TILES], FP16)
        ones = st.sb("ones", [P, PCOLS])
        one_each = st.sb("one_each", [P, 1])
        counted_blocks = st.sb("counted_blocks", [P, 1])
        far = st.sb("far", [P, 1])
        total = st.sb("total", [P, PCOLS])
        upto = st.sb("upto", [P, PCOLS])
        start = st.sb("start", [P, PCOLS], BF16)
        count_i = st.sb("count_i", [P, 1], I32)
        tiles = st.sb("tiles", [P, PARTS])
        tiles_all = st.sb("tiles_all", [P, 1])
        done = st.sb("done", [P, 1])
        done_i = st.sb("done_i", [P, 1], I32)
        left_i = st.sb("left_i", [P, 1], I32)
        full_tiles = st.sb("full_tiles", [P, PARTS])
        first_tile = st.sb("first_tile", [P, PARTS])
        first_edge = st.sb("first_edge", [P, 1])
        first_step = st.sb("first_step", [P, 1])
        shift = st.sb("shift", [P, PARTS])
        shift_step = st.sb("shift_step", [P, PARTS])
        count_tiles = st.sb("count_tiles", [P, STEPS])
        count_tiles_h = st.sb("count_tiles_h", [EP, PART_TILES], FP16)
        lanes_h = st.sb("lanes_h", [EP, P], FP16)
        SLOTS = 5
        COLUMNS = 25
        assert PCOLS % COLUMNS == 0 and COLUMNS % SLOTS == 0
        SCALED = (1, 3, 4)
        PER_TURN, SCALED_PART = COLUMNS // SLOTS * len(SCALED), PCOLS // SLOTS * len(SCALED)
        plain_lane = st.sb("plain_lane", [EP, len(SCALED), P], FP16)
        by_lane = st.sb("by_lane", [EP, SLOTS, 2, P], FP16)
        by_tile = st.sb("by_tile", [EP, SLOTS, PART_TILES], FP16)
        high_sb = st.sb("high_sb", [P, PART_TILES])
        packed = st.sb("packed", [P, PART_TILES])
        TB = -(-PART_TILES // P)
        packed_t = st.sb("packed_t", [P, PARTS, TB, P])
        reached = st.sb("reached", [P, PART_TILES])
        step_of = st.sb("step_of", [P, PARTS * TB])
        QUARTER = STEPS // 4

        def later(row, rows, dt):
            at = member_all[:, row * 2 * STEPS:(row + rows) * 2 * STEPS]
            return at.bitcast(dt).rearrange("p (r s) -> p r s", r=rows)
        goes_to = later(0, 2, FP32)
        final_i, part_i, part2_i = (later(r, 1, I32)[:, 0, :] for r in (2, 3, 4))
        flags = later(5, 2, FP32)[0:1, :, :]
        nowhere = goes_to[0:1, 0, :]
        block_row = st.sb("block_row", [1, STEPS + 2])
        row_tmp = count_tiles[0:1, :]
        bank_row = part_i[0:1, :].bitcast(FP32)

        names = ("loaded zeroed shaped vec is_member counted totals_out placed_start ranked rank_used prefixed "
                 "numbered lane_made scaled slot_made slot_used swept high_out packed_made packed_turned turn_out reach_made step_made "
                 "step_known route_made route_used block_known row_cleared cast masked held held_pe held_act")
        s = {n: st.sem(n) for n in names.split()}
        ps_a, ps_b = st.ps("ps_a", [P, 2, 512]), st.ps("ps_b", [P, 2, 512])
        ps_c, ps_d = st.ps("ps_c", [P, 2, 512]), st.ps("ps_d", [P, 2, 512])
        ps_r = [ps_b[:, 0, :], ps_b[:, 1, :], ps_c[:, 0, :], ps_c[:, 1, :]]
        block = st.block()

        @block.sync
        def _(sp):
            sp.dma_start(src_i[:, :], src.rearrange("(p t) -> p t", p=EP)).then_inc(s["loaded"], 16)
            sp.dma_start(dst_i[:, :], dst.rearrange("(p t) -> p t", p=EP)).then_inc(s["loaded"], 16)

        @block.gpsimd
        def _(pool):
            exact = {"allow_small_or_imprecise_dtypes": True}
            nc.gpsimd.memset(before[:, :], 1.0).then_inc(s["zeroed"], 1)
            nc.gpsimd.memset(one_column[:, :], 0.0).then_inc(s["zeroed"], 1)
            nc.gpsimd.memset(one_each[:, :], 1.0).then_inc(s["zeroed"], 1)
            nc.gpsimd.memset(far[:, :], 0.0).then_inc(s["zeroed"], 1)
            nc.gpsimd.memset(start[:, :], 0.0)
            nc.gpsimd.memset(done[:, :], 0.0)
            nc.gpsimd.memset(zeros_b[:, :], 0.0)
            nc.gpsimd.memset(zeros_h[:, :], 0.0)
            nc.gpsimd.memset(ones[:, :], 1.0)
            nc.gpsimd.iota(count_tiles[:, :], pattern=[[1, STEPS]], base=0, channel_multiplier=0, **exact)
            nc.gpsimd.iota(count_tiles_h[:, :], pattern=[[1, PART_TILES]], base=0, channel_multiplier=0, **exact)
            nc.gpsimd.iota(lanes_h[:, :], pattern=[[1, P]], base=0, channel_multiplier=0, **exact)
            pool.wait_ge(s["zeroed"], 4)
            nc.gpsimd.affine_select(out=before[:, :], in_=before[:, :], compare_op=ALU.is_gt, fill=0.0, base=0,
                                    pattern=[[1, P]], channel_multiplier=-1)
            nc.gpsimd.affine_select(out=step_back[:, :], in_=k["ident"][:, :], compare_op=ALU.not_equal, fill=-1.0,
                                    base=-1, pattern=[[1, P]], channel_multiplier=-1)
            nc.gpsimd.affine_select(out=one_column[:, :], in_=one_column[:, :], compare_op=ALU.not_equal, fill=1.0,
                                    base=-P, pattern=[[1, 2 * P]], channel_multiplier=0)
            nc.gpsimd.affine_select(out=one_each[:, :], in_=one_each[:, :], compare_op=ALU.is_gt, fill=0.0,
                                    base=BLOCKS, pattern=[[0, 1]], channel_multiplier=-1)
            nc.gpsimd.affine_select(out=far[:, :], in_=far[:, :], compare_op=ALU.not_equal, fill=NOWHERE,
                                    base=-BLOCKS, pattern=[[0, 1]], channel_multiplier=1).then_inc(s["shaped"], 1)
            pool.wait_ge(s["shaped"], 1)
            nc.gpsimd.affine_select(out=counted_blocks[:, :], in_=one_each[:, :], compare_op=ALU.is_gt, fill=0.0,
                                    base=0, pattern=[[0, 1]], channel_multiplier=1).then_inc(s["shaped"], 1)
            pool.wait_ge(s["route_used"], PARTS * TB)
            nc.gpsimd.iota(nowhere[:, :], pattern=[[0, STEPS // NOWHERES], [1, NOWHERES]], base=BLOCKS, channel_multiplier=0, **exact)\
                .then_inc(s["shaped"], 1)

        @block.vector
        def _(dve):
            seq = Chain(dve, s["vec"])
            dve.wait_ge(s["shaped"], 2)
            nc.vector.tensor_copy(before_b[:, :], before[0:EP, :]).then_inc(s["cast"], 1)
            nc.vector.tensor_tensor(row_of[:, :, :], column(k["ident"][:, 0:BLOCKS], P), column(k["ident"][:, 64:64 + BLOCKS], P),
                                    ALU.add).then_inc(s["cast"], 1)
            dve.wait_ge(s["loaded"], 32)
            seq.mark(nc.vector.tensor_scalar(scratch_i[:, :], src_i[:, :], 7, None, ALU.logical_shift_right))
            seq.wait()
            seq.mark(nc.vector.tensor_copy(key[:, :], scratch_i[:, :]))
            seq.wait()
            seq.mark(nc.vector.tensor_scalar(scratch_i[:, :], dst_i[:, :], DST_LOW - 1, None, ALU.bitwise_and))
            seq.wait()
            seq.mark(nc.vector.tensor_copy(low[:, :], scratch_i[:, :]))
            seq.wait()
            seq.mark(nc.vector.tensor_scalar(scratch_i[:, :], dst_i[:, :], 10, None, ALU.logical_shift_right))
            seq.wait()
            seq.mark(nc.vector.tensor_scalar(high[:, :], scratch_i[:, :], float(P), float(P), ALU.mult, ALU.add))
            seq.wait()
            seq.mark(nc.vector.tensor_scalar(scratch_i[:, :], src_i[:, :], P - 1, None, ALU.bitwise_and))
            seq.wait()
            seq.mark(nc.vector.tensor_tensor(high[:, :], high[:, :], scratch_i[:, :], ALU.add))
            seq.wait()

            for part in range(PARTS):
                cols = slice(part * PCOLS, (part + 1) * PCOLS)
                if part:
                    dve.wait_ge(s["ranked"], part * BLOCKS)
                def belongs(b):
                    which = k["iota"][0:EP, b:b + 1] if isinstance(b, int) else k["iota"][0:EP, bass.ds(b, 1)]
                    off = b * PCOLS
                    here = member[:, off:off + PCOLS] if isinstance(b, int) else member[:, bass.ds(off, PCOLS)]
                    nc.vector.tensor_scalar(here, key[:, cols], which, None, ALU.is_equal).then_inc(s["is_member"], 1)
                with dve.Fori(0, BLOCKS // UNROLL) as i:
                    for j in range(UNROLL):
                        belongs(i * UNROLL + j)
                belongs(BLOCKS - 1)
                seq.mark(nc.vector.tensor_copy(done_i[:, :], done[:, :]))
                seq.wait()
                seq.mark(nc.vector.tensor_scalar(left_i[:, :], done_i[:, :], P - 1, None, ALU.bitwise_and))
                seq.mark(nc.vector.tensor_scalar(done_i[:, :], done_i[:, :], 7, None, ALU.logical_shift_right))
                seq.wait()
                seq.mark(nc.vector.tensor_copy(full_tiles[:, part:part + 1], done_i[:, :]))
                seq.mark(nc.vector.tensor_copy(first_edge[:, :], left_i[:, :]))
                dve.wait_ge(s["totals_out"], part + 1)
                seq.mark(nc.vector.tensor_tensor_scan(upto[:, :], ones[:, :], total[:, :], 0.0, ALU.mult, ALU.add))
                seq.wait()
                seq.mark(nc.vector.tensor_tensor(done[:, :], done[:, :], upto[:, PCOLS - 1:PCOLS], ALU.add))
                seq.mark(nc.vector.scalar_tensor_tensor(count_i[:, :], upto[:, PCOLS - 1:PCOLS], float(P - 1), first_edge[:, :],
                                                        ALU.add, ALU.add))
                seq.wait()
                seq.mark(nc.vector.tensor_scalar(count_i[:, :], count_i[:, :], 7, None, ALU.arith_shift_right))
                seq.wait()
                nc.vector.tensor_copy(tiles[:, part:part + 1], count_i[:, :]).then_inc(s["counted"], 1)
                seq.mark(nc.vector.tensor_tensor(upto[:, :], upto[:, :], total[:, :], ALU.subtract))
                dve.wait_ge(s["prefixed"], part + 1)
                seq.mark(nc.vector.tensor_copy(first_tile[:, part:part + 1], ps_a[:, 0, 0:1]))
                seq.wait()
                seq.mark(nc.vector.scalar_tensor_tensor(first_edge[:, :], first_tile[:, part:part + 1], float(P), first_edge[:, :],
                                                        ALU.mult, ALU.add))
                seq.wait()
                seq.mark(nc.vector.tensor_scalar(upto[:, :], upto[:, :], first_edge[:, :], None, ALU.add))
                seq.wait()
                seq.mark(nc.vector.tensor_scalar(total[:, :], upto[:, :], 1.0 / 512, MAGIC, ALU.mult, ALU.add))
                seq.wait()
                seq.mark(nc.vector.tensor_scalar(start[0:BLOCKS, :], total[0:BLOCKS, :], -MAGIC, 512.0, ALU.add, ALU.mult))
                seq.wait()
                nc.vector.tensor_tensor(start[64:64 + BLOCKS, :], upto[0:BLOCKS, :], start[0:BLOCKS, :], ALU.subtract)\
                    .then_inc(s["placed_start"], 1)

                def mask_of(b, slot):
                    which = k["iota"][0:EP, b:b + 1] if isinstance(b, int) else k["iota"][0:EP, bass.ds(b, 1)]
                    nc.vector.tensor_scalar(mask[:, slot, :], key[:, cols], which, None, ALU.is_equal).then_inc(s["masked"], 1)

                def take(slot, turn, after_mask):
                    hold(dve, s["ranked"], turn + 1, s["held"])
                    if after_mask:
                        hold(dve, s["masked"], turn + 1, s["held"])
                    hold(dve, s["rank_used"], turn + RANKS, s["held"])
                    nc.vector.copy_predicated(place[:, part, :], mask[:, slot, :], ps_r[slot][0:EP, 0:PCOLS])\
                        .then_inc(s["rank_used"], 1)
                with dve.Fori(0, BLOCKS // UNROLL) as i:
                    mask_of(i * UNROLL, 0)
                    for j in range(UNROLL):
                        if j + 1 < UNROLL:
                            mask_of(i * UNROLL + (j + 1), (j + 1) % RANKS)
                        take(j % RANKS, i * UNROLL + (part * BLOCKS + j), j == 0)
                mask_of(BLOCKS - 1, 0)
                take(0, BLOCKS - 1 + part * BLOCKS, True)

            seq.mark(nc.vector.tensor_scalar(count_i[:, :], done[:, :], float(P - 1), None, ALU.add))
            seq.wait()
            seq.mark(nc.vector.tensor_scalar(count_i[:, :], count_i[:, :], 7, None, ALU.arith_shift_right))
            seq.wait()
            nc.vector.tensor_tensor(tiles_all[:, :], count_i[:, :], one_each[:, :], ALU.max).then_inc(s["counted"], 1)
            dve.wait_ge(s["prefixed"], PARTS + 1)
            seq.mark(nc.vector.tensor_copy(first_step[:, :], ps_a[:, 0, 0:1]))
            seq.mark(nc.vector.tensor_tensor(shift[:, :], full_tiles[:, :], first_tile[:, :], ALU.subtract))
            seq.wait()
            nc.vector.tensor_scalar(shift[:, :], shift[:, :], first_step[:, :], None, ALU.add).then_inc(s["counted"], 1)
            dve.wait_ge(s["prefixed"], PARTS + 2)
            seq.mark(nc.vector.tensor_tensor(shift_step[:, :], ps_a[:, 0, 0:PARTS], far[:, :].to_broadcast([P, PARTS]), ALU.add))
            seq.wait()
            nc.vector.tensor_scalar(goes_to[:, 0, :], count_tiles[:, :], first_step[:, :], None, ALU.is_ge)\
                .then_inc(s["counted"], 1)

            for part in range(PARTS):
                seq.mark(nc.vector.tensor_copy(place_i[:, :], place[:, part, :]))
                seq.wait()
                seq.mark(nc.vector.tensor_scalar(scratch_i[:, 0:PCOLS], place_i[:, :], P - 1, None, ALU.bitwise_and))
                seq.mark(nc.vector.tensor_scalar(place_i[:, :], place_i[:, :], 7, None, ALU.logical_shift_right))
                seq.wait()
                seq.mark(nc.vector.tensor_copy(lane[:, :], scratch_i[:, 0:PCOLS]))
                seq.mark(nc.vector.tensor_copy(tile[:, :], place_i[:, :]))
                seq.wait()
                with dve.Fori(0, PCOLS // COLUMNS) as i:
                    for j in range(COLUMNS):
                        n = i * COLUMNS + j
                        slot = j % SLOTS
                        at = bass.ds(n, 1)
                        value_at = bass.ds(n + part * PCOLS, 1)
                        dve.wait_ge(s["slot_used"], n + part * PCOLS + 1)
                        if slot in SCALED:
                            nc.vector.tensor_scalar(plain_lane[:, SCALED.index(slot), :], lanes_h[:, :], lane[:, at], None,
                                                    ALU.is_equal).then_inc(s["lane_made"], 1)
                        else:
                            nc.vector.tensor_scalar(by_lane[:, slot, 0, :], lanes_h[:, :], lane[:, at], low[:, value_at],
                                                    ALU.is_equal, ALU.mult)
                            nc.vector.tensor_scalar(by_lane[:, slot, 1, :], lanes_h[:, :], lane[:, at], high[:, value_at],
                                                    ALU.is_equal, ALU.mult)
                        nc.vector.tensor_scalar(by_tile[:, slot, :], count_tiles_h[:, :], tile[:, at], None, ALU.is_equal)\
                            .then_inc(s["slot_made"], 1)
                dve.wait_ge(s["high_out"], part + 1)
                if part:
                    dve.wait_ge(s["packed_turned"], part * TB)
                nc.vector.scalar_tensor_tensor(packed[:, :], high_sb[:, :], float(DST_LOW), ps_a[:, part % 2, 0:PART_TILES],
                                               ALU.mult, ALU.add).then_inc(s["packed_made"], 1)
                nc.vector.tensor_scalar(reached[:, :], count_tiles[:, 0:PART_TILES], first_tile[:, part:part + 1], None,
                                        ALU.is_ge).then_inc(s["reach_made"], 1)
                dve.wait_ge(s["step_known"], part + 1)
                for t in range(TB):
                    n = part * TB + t
                    w = min(P, PART_TILES - t * P)
                    seq.mark(nc.vector.tensor_scalar(step_of[0:w, n:n + 1], ps_d[0:w, part % 2, t:t + 1], k["iota_p"][0:w, :],
                                                     float(t * P), ALU.add, ALU.add))
                seq.wait()

            dve.wait_ge(s["step_made"], 1)
            for n in range(PARTS * TB):
                w = min(P, PART_TILES - n % TB * P)
                if n >= 2:
                    dve.wait_ge(s["route_used"], n - 1)
                nc.vector.tensor_scalar(goes_to[0:w, n % 2, :], count_tiles[0:w, :], step_of[0:w, n:n + 1], None,
                                        ALU.is_equal).then_inc(s["route_made"], 1)

            dve.wait_ge(s["route_used"], PARTS * TB)
            seq.mark(nc.vector.tensor_copy(final_i[:, 0:2 * QUARTER].rearrange("p (q t) -> p q t", q=2), ps_a[:, :, 0:QUARTER]))
            seq.mark(nc.vector.tensor_copy(final_i[:, 2 * QUARTER:].rearrange("p (q t) -> p q t", q=2), ps_b[:, :, 0:QUARTER]))
            seq.wait()
            seq.mark(nc.vector.tensor_scalar(part_i[:, :], final_i[:, :], 17, None, ALU.logical_shift_right))
            seq.mark(nc.vector.tensor_scalar(part2_i[:, :], final_i[:, :], DST_LOW - 1, None, ALU.bitwise_and))
            seq.wait()
            seq.mark(nc.vector.tensor_scalar(count_tiles[:, :], part_i[:, :], -1.0, 0.0, ALU.add, ALU.max))
            seq.wait()
            seq.mark(nc.vector.scalar_tensor_tensor(node_of[:, :], count_tiles[:, :], float(DST_LOW), part2_i[:, :],
                                                    ALU.mult, ALU.add))
            seq.wait()
            seq.mark(nc.vector.tensor_scalar(part2_i[:, :], final_i[:, :], 10, P - 1, ALU.logical_shift_right, ALU.bitwise_and))
            seq.mark(nc.vector.tensor_scalar(count_tiles[:, :], part_i[:, :], 0.0, NO_NODE, ALU.is_equal, ALU.mult))
            seq.wait()
            seq.mark(nc.vector.tensor_tensor(local_of[:, :], count_tiles[:, :], part2_i[:, :], ALU.add))
            dve.wait_ge(s["block_known"], 2)
            seq.wait()
            blocks = block_row[:, 1:STEPS + 1]
            seq.mark(nc.vector.tensor_tensor(flags[:, 0, :], blocks, block_row[:, 0:STEPS], ALU.not_equal))
            seq.mark(nc.vector.tensor_tensor(flags[:, 1, :], blocks, block_row[:, 2:STEPS + 2], ALU.not_equal))
            seq.mark(nc.vector.tensor_scalar(bank_row[:, :], blocks, -1.0, 1.0 / SUM_BANKS, ALU.add, ALU.mult))
            seq.wait()
            seq.mark(nc.vector.tensor_scalar(bank_row[:, :], bank_row[:, :], MAGIC, None, ALU.add))
            seq.wait()
            seq.mark(nc.vector.tensor_scalar(bank_row[:, :], bank_row[:, :], -MAGIC, -float(SUM_BANKS), ALU.add, ALU.mult))
            seq.wait()
            seq.mark(nc.vector.tensor_tensor(bank_row[:, :], bank_row[:, :], blocks, ALU.add))
            for_pe = step_info[0:1, :].rearrange("p (s f) -> p s f", f=2)
            for_act = step_info[32:33, :].rearrange("p (s f) -> p s f", f=2)
            seq.mark(nc.vector.tensor_copy(step_info[64:65, 0:STEPS], blocks))
            seq.wait()
            seq.mark(nc.vector.tensor_copy(for_pe[:, :, 0], bank_row[:, :]))
            dve.wait_ge(s["shaped"], 3)
            for info, value, other, flag in ((for_pe[:, :, 1], bank_row[:, :], IDLE_BANK, 0),
                                             (for_act[:, :, 0], bank_row[:, :], SPARE_BANK, 1)):
                seq.mark(nc.vector.scalar_tensor_tensor(row_tmp[:, :], value, -float(other), flags[:, flag, :],
                                                        ALU.add, ALU.mult))
                seq.wait()
                seq.mark(nc.vector.tensor_scalar(info, row_tmp[:, :], float(other), None, ALU.add))
                seq.wait()
            seq.mark(nc.vector.tensor_tensor(row_tmp[:, :], blocks, nowhere, ALU.subtract))
            seq.wait()
            seq.mark(nc.vector.tensor_tensor(row_tmp[:, :], row_tmp[:, :], flags[:, 1, :], ALU.mult))
            seq.wait()
            seq.mark(nc.vector.tensor_tensor(for_act[:, :, 1], row_tmp[:, :], nowhere, ALU.add))

        @block.scalar
        def _(act):
            nc.scalar.activation(block_row[:, :], k["iota"][0:1, 0:1].to_broadcast([1, STEPS + 2]), ACT.Copy, bias=-1.0)\
                .then_inc(s["row_cleared"], 1)
            for part in range(PARTS):
                act.wait_ge(s["numbered"], part + 1)
                nc.scalar.activation(total[:, :], ps_d[:, 0, 0:PCOLS], ACT.Copy).then_inc(s["totals_out"], 1)
            act.wait_ge(s["step_made"], 1)
            act.wait_ge(s["row_cleared"], 1)
            for h, ps in enumerate((ps_c, ps_d)):
                nc.scalar.activation(block_row[:, 1 + 2 * h * QUARTER:1 + 2 * (h + 1) * QUARTER]
                                     .rearrange("p (q t) -> p q t", q=2), ps[0:1, :, 0:QUARTER], ACT.Copy)\
                    .then_inc(s["block_known"], 1)
            for part in range(PARTS):
                with act.Fori(0, PCOLS // COLUMNS) as i:
                    for j in range(COLUMNS):
                        if j % SLOTS in SCALED:
                            here, slot = SCALED.index(j % SLOTS), j % SLOTS
                            n = j // SLOTS * len(SCALED) + here
                            hold(act, s["lane_made"], i * PER_TURN + (part * SCALED_PART + n + 1), s["held_act"])
                            value_at = bass.ds(i * COLUMNS + (part * PCOLS + j), 1)
                            nc.scalar.activation(by_lane[:, slot, 0, :], plain_lane[:, here, :], ACT.Copy, scale=low[:, value_at])
                            nc.scalar.activation(by_lane[:, slot, 1, :], plain_lane[:, here, :], ACT.Copy,
                                                 scale=high[:, value_at]).then_inc(s["scaled"], 1)
                act.wait_ge(s["swept"], part + 1)
                if part:
                    act.wait_ge(s["packed_made"], part)
                nc.scalar.activation(high_sb[:, :], ps_b[:, part % 2, 0:PART_TILES], ACT.Copy).then_inc(s["high_out"], 1)
                for t in range(TB):
                    w = min(P, PART_TILES - t * P)
                    act.wait_ge(s["packed_turned"], part * TB + t + 1)
                    nc.scalar.activation(packed_t[0:w, part, t, :], ps_c[0:w, (part * TB + t) % 2, 0:P], ACT.Copy)\
                        .then_inc(s["turn_out"], 1)

        @block.tensor
        def _(pe):
            pe.sem_inc(s["slot_used"], SLOTS)
            pe.sem_inc(s["rank_used"], RANKS)
            pe.wait_ge(s["shaped"], 2)
            pe.wait_ge(s["cast"], 2)

            for part in range(PARTS):
                if part:
                    pe.wait_ge(s["totals_out"], part)
                nc.tensor.matmul(ps_d[:, 0, 0:PCOLS], zeros_b[0:EP, 0:P], zeros_b[0:EP, :], start=True, stop=False)

                def count(b):
                    off = b * PCOLS
                    here = member[:, off:off + PCOLS] if isinstance(b, int) else member[:, bass.ds(off, PCOLS)]
                    to_row = one_column[:, P - b:2 * P - b] if isinstance(b, int) else one_column[:, bass.ds(P - b, P)]
                    nc.tensor.matmul(ps_d[:, 0, 0:PCOLS], to_row, here, start=False, stop=False)
                with pe.Fori(0, BLOCKS // UNROLL) as i:
                    for j in range(UNROLL):
                        if j % RANKS == 0:
                            hold(pe, s["is_member"], i * UNROLL + (part * BLOCKS + j + RANKS), s["held_pe"])
                        count(i * UNROLL + j)
                hold(pe, s["is_member"], (part + 1) * BLOCKS, s["held_pe"])
                count(BLOCKS - 1)
                nc.tensor.matmul(ps_d[:, 0, 0:PCOLS], zeros_b[0:EP, 0:P], zeros_b[0:EP, :], start=False, stop=True)\
                    .then_inc(s["numbered"], 1)
                pe.wait_ge(s["counted"], part + 1)
                nc.tensor.matmul(ps_a[:, 0, 0:1], before[:, :], tiles[:, part:part + 1], start=True, stop=True)\
                    .then_inc(s["prefixed"], 1)
                pe.wait_ge(s["placed_start"], part + 1)
                if part:
                    pe.wait_ge(s["rank_used"], part * BLOCKS + RANKS)

                def rank(b, slot, turn):
                    hold(pe, s["rank_used"], turn + 1, s["held_pe"])
                    off = b * PCOLS
                    here = member[:, off:off + PCOLS] if isinstance(b, int) else member[:, bass.ds(off, PCOLS)]
                    row = row_of[:, b, :] if isinstance(b, int) else \
                        row_of[:, bass.ds(b, 1), :].rearrange("p o j -> p (o j)")
                    nc.tensor.matmul(ps_r[slot][:, 0:PCOLS], before_b[:, :], here, start=True, stop=False)
                    nc.tensor.matmul(ps_r[slot][:, 0:PCOLS], row, start[:, :], start=False, stop=True).then_inc(s["ranked"], 1)
                with pe.Fori(0, BLOCKS // UNROLL) as i:
                    for j in range(UNROLL):
                        rank(i * UNROLL + j, j % RANKS, i * UNROLL + (part * BLOCKS + j))
                rank(BLOCKS - 1, 0, BLOCKS - 1 + part * BLOCKS)

            pe.wait_ge(s["counted"], PARTS + 1)
            nc.tensor.matmul(ps_a[:, 0, 0:1], before[:, :], tiles_all[:, :], start=True, stop=True).then_inc(s["prefixed"], 1)
            pe.wait_ge(s["counted"], PARTS + 2)
            nc.tensor.matmul(ps_a[:, 0, 0:PARTS], step_back[:, :], shift[:, :], start=True, stop=True)\
                .then_inc(s["prefixed"], 1)
            pe.wait_ge(s["counted"], PARTS + 3)
            for q in range(4):
                ins = nc.tensor.matmul((ps_c, ps_d)[q // 2][0:1, q % 2, 0:QUARTER], counted_blocks[:, :],
                                       goes_to[:, 0, q * QUARTER:(q + 1) * QUARTER], start=True, stop=True)
            ins.then_inc(s["step_made"], 1)

            for part in range(PARTS):
                if part >= 2:
                    pe.wait_ge(s["packed_made"], part - 1)
                    pe.wait_ge(s["high_out"], part - 1)
                both_numbers = [ps[:, part % 2, 0:PART_TILES] for ps in (ps_a, ps_b)]
                for ps in both_numbers:
                    nc.tensor.matmul(ps, zeros_h[:, 0:P], zeros_h[:, :], start=True, stop=False)
                with pe.Fori(0, PCOLS // COLUMNS) as i:
                    for j in range(COLUMNS):
                        slot = j % SLOTS
                        pe.wait_ge(s["slot_made"], i * COLUMNS + (part * PCOLS + j + 1))
                        if slot in SCALED:
                            pe.wait_ge(s["scaled"], i * PER_TURN + (part * SCALED_PART + j // SLOTS * len(SCALED)
                                                                    + SCALED.index(slot) + 1))
                        for number, ps in enumerate(both_numbers):
                            ins = nc.tensor.matmul(ps, by_lane[:, slot, number, :], by_tile[:, slot, :], start=False, stop=False)
                        ins.then_inc(s["slot_used"], 1)
                for ps in both_numbers:
                    ins = nc.tensor.matmul(ps, zeros_h[:, 0:P], zeros_h[:, :], start=False, stop=True)
                ins.then_inc(s["swept"], 1)
                pe.wait_ge(s["packed_made"], part + 1)
                if part == 0:
                    pe.wait_ge(s["block_known"], 2)
                for t in range(TB):
                    n = part * TB + t
                    w = min(P, PART_TILES - t * P)
                    if n >= 2:
                        pe.wait_ge(s["turn_out"], n - 1)
                    nc.tensor.transpose(ps_c[0:w, n % 2, 0:P], packed[:, t * P:t * P + w], k["ident"][:, :])\
                        .then_inc(s["packed_turned"], 1)
                pe.wait_ge(s["reach_made"], part + 1)
                for t in range(TB):
                    w = min(P, PART_TILES - t * P)
                    ins = nc.tensor.matmul(ps_d[0:w, part % 2, t:t + 1], reached[:, t * P:t * P + w], shift_step[:, part:part + 1],
                                           start=True, stop=True)
                ins.then_inc(s["step_known"], 1)

            pe.wait_ge(s["turn_out"], PARTS * TB)
            for n in range(PARTS * TB):
                w = min(P, PART_TILES - n % TB * P)
                pe.wait_ge(s["route_made"], n + 1)
                for q in range(4):
                    ins = nc.tensor.matmul((ps_a, ps_b)[q // 2][:, q % 2, 0:QUARTER], packed_t[0:w, n // TB, n % TB, :],
                                           goes_to[0:w, n % 2, q * QUARTER:(q + 1) * QUARTER],
                                           start=n == 0, stop=n == PARTS * TB - 1)
                ins.then_inc(s["route_used"], 1)


TURN_AT, KEEP_AT, WEIGH_AT, SCORES_AT = 0, 1, 2, 3


def aggregate(nc, sems, k, name, table, row, width, heads, s_src, node_of, local_of, step_info, sums_of, loads=()):
    with ExitStack() as ctx:
        st = Stage(nc, ctx, sems, name)
        rows = st.sb("rows", [P, RING, GROUP, row])
        target = st.sb("target", [P, RING, GROUP], I32)
        hot = st.sb("hot", [P, RING, GROUP, P])
        hot_t = st.sb("hot_t", [P, GROUP, P])
        score = st.sb("score", [P, 3, GROUP, heads])
        weight = st.sb("weight", [P, 3, GROUP, heads])
        weighted_hot = st.sb("weighted_hot", [P, 2, GROUP, P]) if heads == 1 else None
        zeros = st.sb("zeros", [P, 512], BF16)
        banks = st.ps("banks", [P, (SUM_BANKS + 2) * 512])
        ps_t = st.ps("ps_t", [P, GROUP, P])
        ps_s = st.ps("ps_s", [P, 2, 512])
        names = ("zeroed target_ready held_pool held_act is_hot turned turn_kept scored added leaky is_weight ready "
                 "summed taken loaded")
        s = {n: st.sem(n) for n in names.split()}
        gathered = [st.sem(f"gathered{u}") for u in range(RING)]
        AHEAD = 2 if heads > 1 else 1
        FREE = RING * GROUP
        block = st.block()

        def rounds(eng, body):
            with eng.Fori(0, ROUNDS) as r:
                for u in range(RING):
                    body(r * RING + u, r, u)
            for g in range(ROUNDS * RING, GROUPS):
                body(g, g // RING, g % RING)

        def exists(g, ahead):
            return not isinstance(g, int) or g + ahead < GROUPS

        def cols(at, n):
            return slice(at, at + n) if isinstance(at, int) else bass.ds(at, n)

        @block.sync
        def _(sp):
            for there, here in loads:
                sp.dma_start(there, here).then_inc(s["loaded"], 16)
            if loads:
                sp.wait_ge(s["loaded"], 16 * len(loads))

        @block.gpsimd
        def _(pool):
            def body(g, r, u):
                hold(pool, s["target_ready"], g + 1, s["held_pool"])
                for j in range(GROUP):
                    nc.gpsimd.indirect_dma_start(
                        out=rows[:, u, j, :], out_offset=None, in_=table[:, :],
                        in_offset=bass.IndirectOffsetOnAxis(ap=target[:, u, j:j + 1], axis=0)).then_inc(gathered[u], 16)
            rounds(pool, body)

        @block.vector
        def _(dve):
            nc.vector.memset(zeros[:, :], 0.0).then_inc(s["zeroed"], 1)

            def copy_targets(g, u):
                nc.vector.tensor_copy(target[:, u, :], node_of[:, cols(g * GROUP, GROUP)]).then_inc(s["target_ready"], 1)

            def make_hot(g, u):
                nc.vector.tensor_tensor(hot[:, u, :, :], middle(k["iota"][:, :], GROUP),
                                        column(local_of[:, cols(g * GROUP, GROUP)], P), ALU.is_equal).then_inc(s["is_hot"], 1)

            def add_scores(g, r, u):
                dve.wait_ge(s["scored"], g + 1)
                dve.wait_ge(gathered[u], r * (16 * GROUP) + 16 * GROUP)
                nc.vector.tensor_tensor(score[:, u % 3, :, :],
                                        ps_s[:, u % 2, 0:GROUP * heads].rearrange("p (j h) -> p j h", h=heads),
                                        rows[:, u, :, width:width + heads], ALU.add).then_inc(s["added"], 1)
                dve.wait_ge(s["added"], g + 1)
                flat = score[:, u % 3, :, :].rearrange("p j h -> p (j h)")
                nc.vector.scalar_tensor_tensor(flat, flat, SLOPE, flat, ALU.mult, ALU.max).then_inc(s["leaky"], 1)

            for u in range(RING - 1):
                copy_targets(u, u)
            for u in range(AHEAD + 2):
                make_hot(u, u)
            for u in range(AHEAD):
                add_scores(u, 0, u)

            def body(g, r, u):
                dve.wait_ge(s["is_weight"], g + 1)
                for j in range(GROUP):
                    if heads == 1:
                        if j == 0:
                            dve.wait_ge(s["summed"], g * GROUP + (FREE - GROUP))
                        nc.vector.tensor_scalar(weighted_hot[:, u % 2, j, :], hot[:, u, j, :], weight[:, u % 3, j, :], None,
                                                ALU.mult).then_inc(s["ready"], 1)
                    else:
                        by_head = rows[:, u, j, 0:width].rearrange("p (h d) -> p h d", h=heads)
                        nc.vector.tensor_tensor(by_head, by_head, column(weight[:, u % 3, j, :], width // heads),
                                                ALU.mult).then_inc(s["ready"], 1)
                if exists(g, AHEAD):
                    add_scores(g + AHEAD, r + (u + AHEAD) // RING, (u + AHEAD) % RING)
                if exists(g, AHEAD + 2):
                    dve.wait_ge(s["summed"], g * GROUP + (FREE - (RING - AHEAD - 3) * GROUP))
                    make_hot(g + AHEAD + 2, (u + AHEAD + 2) % RING)
                if not (isinstance(g, int) and g == 0) and exists(g, RING - 1):
                    dve.wait_ge(s["summed"], g * GROUP + FREE)
                    copy_targets(g + RING - 1, (u + RING - 1) % RING)
            rounds(dve, body)

        @block.scalar
        def _(act):
            act.sem_inc(s["taken"], SUM_BANKS)

            def keep_turn(g):
                act.wait_ge(s["turned"], g + 1)
                if not (isinstance(g, int) and g == 0):
                    act.wait_ge(s["scored"], g)
                nc.scalar.activation(hot_t[:, :, :], ps_t[:, :, :], ACT.Copy).then_inc(s["turn_kept"], 1)

            def weigh(g, u):
                act.wait_ge(s["leaky"], g + 1)
                nc.scalar.activation(weight[:, u % 3, :, :], score[:, u % 3, :, :], ACT.Exp, scale=-1.0)\
                    .then_inc(s["is_weight"], 1)

            def load_step(step):
                _, (bank, place) = nc.values_load_multi_w_load_instructions(
                    step_info[32:33, cols(step * 2, 2)], engines=(mybir.EngineType.Activation,), min_val=0,
                    max_val=BLOCKS + NOWHERES - 1, skip_runtime_bounds_check_because="the sort writes them within bounds")
                return nc.s_assert_within(bank, 0, SPARE_BANK, skip_runtime_bounds_check_because="a bank number"), place

            for g in range(AHEAD + 1):
                keep_turn(g)
            for g in range(AHEAD):
                weigh(g, g)

            def body(g, r, u):
                for j in range(GROUP):
                    step = g * GROUP + j
                    bank, place = load_step(step)
                    hold(act, s["summed"], step + (FREE + 1), s["held_act"])
                    if j % 2 == 0:
                        hold(act, s["taken"], step + (SUM_BANKS - 2), s["held_act"])
                    nc.scalar.activation(sums_of[:, bass.ds(place * width, width)], banks[:, bass.ds(bank * 512, width)],
                                         ACT.Copy).then_inc(s["taken"], 1)
                    if j == KEEP_AT and exists(g, AHEAD + 1):
                        keep_turn(g + AHEAD + 1)
                    if j == WEIGH_AT and exists(g, AHEAD):
                        weigh(g + AHEAD, u + AHEAD)
            rounds(act, body)

        @block.tensor
        def _(pe):
            pe.sem_inc(s["summed"], FREE)
            pe.wait_ge(s["zeroed"], 1)
            for b in range(SUM_BANKS + 2):
                nc.tensor.matmul(banks[:, b * 512:(b + 1) * 512], zeros[:, 0:P], zeros[:, :], start=True, stop=True)

            def turn(g, u):
                pe.wait_ge(s["is_hot"], g + 1)
                if not (isinstance(g, int) and g == 0):
                    pe.wait_ge(s["turn_kept"], g)
                for j in range(GROUP):
                    ins = nc.tensor.transpose(ps_t[:, j, :], hot[:, u, j, :], k["ident"][:, :])
                ins.then_inc(s["turned"], 1)

            def load_blocks(g):
                _, blocks = nc.values_load_multi_w_load_instructions(
                    step_info[64:65, cols(g * GROUP, GROUP)], engines=(mybir.EngineType.PE,), min_val=0, max_val=BLOCKS - 1,
                    skip_runtime_bounds_check_because="the sort writes them within bounds")
                return blocks

            def source_scores(g, u, blocks):
                pe.wait_ge(s["turn_kept"], g + 1)
                if not (isinstance(g, int) and g < 2):
                    pe.wait_ge(s["added"], g - 1)
                for j in range(GROUP):
                    ins = nc.tensor.matmul(ps_s[:, u % 2, j * heads:(j + 1) * heads], hot_t[:, j, :],
                                           s_src[:, bass.ds(blocks[j] * heads, heads)], start=True, stop=True)
                ins.then_inc(s["scored"], 1)

            def load_step(step):
                _, banks_of = nc.values_load_multi_w_load_instructions(
                    step_info[0:1, cols(step * 2, 2)], engines=(mybir.EngineType.PE,), min_val=0, max_val=IDLE_BANK,
                    skip_runtime_bounds_check_because="the sort writes them within bounds")
                return banks_of

            for g in range(AHEAD + 1):
                turn(g, g)
                source_scores(g, g, load_blocks(g))

            def body(g, r, u):
                for j in range(GROUP):
                    step = g * GROUP + j
                    bank, cleared = load_step(step)
                    pe.wait_ge(s["taken"], step + 1)
                    nc.tensor.matmul(banks[:, bass.ds(cleared * 512, 2)], zeros[:, 0:P], zeros[:, 0:2],
                                     start=True, stop=True, skip_group_check=True)
                    pe.wait_ge(s["ready"], step + 1)
                    by_source = hot[:, u, j, :] if heads > 1 else weighted_hot[:, u % 2, j, :]
                    nc.tensor.matmul(banks[:, bass.ds(bank * 512, width)], by_source, rows[:, u, j, 0:width],
                                     start=False, stop=True, skip_group_check=True).then_inc(s["summed"], 1)
                    if exists(g, AHEAD + 1):
                        if j == TURN_AT:
                            turn(g + AHEAD + 1, (u + AHEAD + 1) % RING)
                        if j == SCORES_AT:
                            source_scores(g + AHEAD + 1, u + AHEAD + 1, load_blocks(g + AHEAD + 1))
            rounds(pe, body)


def project_out(nc, sems, k, sums1, g_heads, beta_heads, w_out, b_out, a_out, table2, s_src2):
    with ExitStack() as ctx:
        st = Stage(nc, ctx, sems, "mid")
        NORMS = CHUNK_BLOCKS * HEADS
        WIDE = CHUNK_BLOCKS * HD
        OUT = FEAT + 2
        RQ, KQ = FEAT // P, HD // P
        centred = st.sb("centred", [P, WIDE])
        normed = st.sb("normed", [P, WIDE])
        elu = st.sb("elu", [P, WIDE])
        mean, spread = st.sb("mean", [P, NORMS]), st.sb("spread", [P, NORMS])
        g_row, beta_row = st.sb("g_row", [P, HD]), st.sb("beta_row", [P, HD])
        w_rows = st.sb("w_rows", [P, RQ, HD])
        w_t = st.sb("w_t", [P, KQ, OUT])
        a_cols = st.sb("a_cols", [P, RQ, 2])
        b_col = st.sb("b_col", [P, RQ])
        b_wide = st.sb("b_wide", [P, RQ, P])
        b_row = st.sb("b_row", [P, OUT])
        turned_sb = st.sb("turned_sb", [P, 2, HD])
        rows = st.sb("rows", [P, 2, ROW2])
        ps_t, ps_h = st.ps("ps_t", [P, 2, HD]), st.ps("ps_h", [P, 2, 512])
        ps_w = st.ps("ps_w", [P, 2, 512])
        names = ("w_loaded b_loaded g_loaded vec pool_seq is_centred is_squared var_ready std_ready is_normed is_affine "
                 "is_exp is_elu b_widened w_turned w_kept wa_made wa_kept turned turn_kept products rows_made")
        s = {n: st.sem(n) for n in names.split()}
        stored = [st.sem("stored0"), st.sem("stored1")]
        VEC = 8
        SPLIT = (CHUNK_BLOCKS + 1) // 2
        PARTS_OF = ((0, SPLIT), (SPLIT, CHUNK_BLOCKS))
        block = st.block()

        def both(eng, chunk):
            with eng.Fori(0, CHUNKS - 1) as c:
                chunk(c)
            chunk(CHUNKS - 1)

        def part_of(ap, part, width=HD):
            return ap[:, PARTS_OF[part][0] * width:PARTS_OF[part][1] * width]

        def by_norm(ap):
            return ap.rearrange("p (n d) -> p n d", d=HDIM)

        def by_block(ap):
            return ap.rearrange("p (b f) -> p b f", f=HD)

        @block.sync
        def _(sp):
            sp.dma_start(w_rows[:, :, :], w_out.rearrange("(q p) f -> p q f", p=P)).then_inc(s["w_loaded"], 16)
            for side in range(2):
                part = a_out[(1 - side) * FEAT:(2 - side) * FEAT]
                sp.dma_start(a_cols[:, :, side], part.rearrange("(q p) -> p q", p=P),
                             allow_slow_non_contiguous=True).then_inc(s["w_loaded"], 16)
            sp.dma_start(b_col[:, :], b_out.rearrange("(q p) -> p q", p=P), allow_slow_non_contiguous=True)\
                .then_inc(s["b_loaded"], 16)
            sp.dma_start(b_row[:, 0:FEAT], b_out.partition_broadcast(P)).then_inc(s["b_loaded"], 16)
            sp.dma_start(g_row[:, :], g_heads.rearrange("h d -> (h d)").partition_broadcast(P)).then_inc(s["g_loaded"], 16)
            sp.dma_start(beta_row[:, :], beta_heads.rearrange("h d -> (h d)").partition_broadcast(P)).then_inc(s["g_loaded"], 16)
            for x in stored:
                sp.sem_inc(x, 16)

            def chunk(c):
                last = isinstance(c, int)
                for b in range(CHUNK_BLOCKS):
                    sp.wait_ge(s["rows_made"], c * CHUNK_BLOCKS + b + 1)
                    n = LAST if last and b == CHUNK_BLOCKS - 1 else P
                    first = c * (CHUNK_BLOCKS * P) + b * P
                    at = slice(first, first + n) if last else bass.ds(first, n)
                    sp.dma_start(table2[at, :], rows[0:n, b % 2, :]).then_inc(stored[b % 2], 16)
            both(sp, chunk)
            for half, uses in ((0, CHUNKS * 4), (1, CHUNKS * 3)):
                sp.wait_ge(stored[half], 16 * (uses + 1))

        @block.gpsimd
        def _(pool):
            pool.wait_ge(s["g_loaded"], 32)

            def chunk(c):
                for part, (start, end) in enumerate(PARTS_OF):
                    here = by_block(part_of(normed, part))
                    pool.wait_ge(s["is_normed"], c * 2 + (part + 1))
                    nc.gpsimd.tensor_tensor(here, here, middle(g_row[:, :], end - start), ALU.mult).then_inc(s["pool_seq"], 1)
                    pool.wait_ge(s["pool_seq"], c * 2 + (part + 1))
                    nc.gpsimd.tensor_tensor(here, here, middle(beta_row[:, :], end - start), ALU.add)\
                        .then_inc(s["is_affine"], 1)
            both(pool, chunk)

        @block.vector
        def _(dve):
            nc.vector.memset(rows[:, :, :], 0.0).then_inc(s["b_widened"], 1)
            dve.wait_ge(s["b_loaded"], 32)
            nc.vector.tensor_copy(b_wide[:, :, :], column(b_col[:, :], P)).then_inc(s["b_widened"], 1)
            dve.wait_ge(s["wa_kept"], KQ + 1)

            def rows_of(c, b):
                g = c * CHUNK_BLOCKS + b
                dve.wait_ge(s["products"], g + 1)
                dve.wait_ge(stored[b % 2], (c * (4 if b % 2 == 0 else 3) + b // 2) * 16 + 16)
                nc.vector.tensor_tensor(rows[:, b % 2, 0:FEAT + 1], ps_h[:, b % 2, 0:FEAT + 1], b_row[:, 0:FEAT + 1], ALU.add)
                at = slice(g, g + 1) if isinstance(g, int) else bass.ds(g, 1)
                nc.vector.tensor_tensor(s_src2[:, at], ps_h[:, b % 2, FEAT + 1:OUT], b_row[:, FEAT + 1:OUT], ALU.add)\
                    .then_inc(s["rows_made"], 1)

            def normalise(c, before=None):
                seq = Chain(dve, s["vec"], c * VEC)
                sums = []
                for part, (start, end) in enumerate(PARTS_OF):
                    off, size = c * WIDE + start * HD, (end - start) * HD
                    sums.append(by_norm(sums1[:, off:off + size] if isinstance(c, int) else sums1[:, bass.ds(off, size)]))
                    seq.mark(nc.vector.tensor_reduce(part_of(mean, part, HEADS), sums[part], AX.X, ALU.add))
                    seq.wait()
                    seq.mark(nc.vector.tensor_scalar(part_of(mean, part, HEADS), part_of(mean, part, HEADS), 1.0 / HDIM, None,
                                                     ALU.mult))
                    seq.wait()
                    nc.vector.tensor_tensor(by_norm(part_of(centred, part)), sums[part],
                                            column(part_of(mean, part, HEADS), HDIM), ALU.subtract).then_inc(s["is_centred"], 1)
                for part in range(2):
                    if before is not None:
                        rows_of(before, part)
                    dve.wait_ge(s["is_squared"], c * 2 + (part + 1))
                    nc.vector.tensor_reduce(part_of(spread, part, HEADS), by_norm(part_of(normed, part)), AX.X, ALU.add)\
                        .then_inc(s["var_ready"], 1)
                for part in range(2):
                    if before is not None:
                        rows_of(before, 2 + part)
                    dve.wait_ge(s["std_ready"], c * 2 + (part + 1))
                    seq.mark(nc.vector.reciprocal(part_of(spread, part, HEADS), part_of(spread, part, HEADS)))
                    seq.wait()
                    nc.vector.tensor_tensor(by_norm(part_of(normed, part)), by_norm(part_of(centred, part)),
                                            column(part_of(spread, part, HEADS), HDIM), ALU.mult).then_inc(s["is_normed"], 1)
                return seq

            def make_elu(c, seq):
                for part in range(2):
                    dve.wait_ge(s["is_exp"], c * 2 + (part + 1))
                    seq.mark(nc.vector.tensor_scalar(part_of(centred, part), part_of(centred, part), 1.0, -1.0, ALU.min, ALU.add))
                    seq.wait()
                    nc.vector.scalar_tensor_tensor(part_of(elu, part), part_of(normed, part), 0.0, part_of(centred, part),
                                                   ALU.max, ALU.add).then_inc(s["is_elu"], 1)
                assert seq.n == VEC

            make_elu(0, normalise(0))

            def chunk(c):
                last = isinstance(c, int)
                seq = None if last else normalise(c + 1, c)
                for b in range(0 if last else 4, CHUNK_BLOCKS):
                    rows_of(c, b)
                if not last:
                    make_elu(c + 1, seq)
            both(dve, chunk)

        @block.scalar
        def _(act):
            for q in range(KQ):
                act.wait_ge(s["w_turned"], 1)
                nc.scalar.activation(w_t[:, q, 0:FEAT], (ps_t, ps_h)[q // 2][:, q % 2, 0:FEAT], ACT.Copy).then_inc(s["w_kept"], 1)
            act.wait_ge(s["wa_made"], 1)
            for q in range(KQ):
                nc.scalar.activation(w_t[:, q, FEAT:OUT], ps_w[:, 0, 2 * q:2 * q + 2], ACT.Copy).then_inc(s["wa_kept"], 1)
            nc.scalar.activation(b_row[:, FEAT:OUT], ps_w[:, 1, 0:2], ACT.Copy).then_inc(s["wa_kept"], 1)

            def square(c, part):
                act.wait_ge(s["is_centred"], c * 2 + (part + 1))
                nc.scalar.activation(part_of(normed, part), part_of(centred, part), ACT.Square).then_inc(s["is_squared"], 1)

            def spread_of(c, part):
                act.wait_ge(s["var_ready"], c * 2 + (part + 1))
                nc.scalar.activation(part_of(spread, part, HEADS), part_of(spread, part, HEADS), ACT.Sqrt, bias=k["eps"][:, :],
                                     scale=1.0 / HDIM).then_inc(s["std_ready"], 1)

            def exp_of(c, part):
                act.wait_ge(s["is_affine"], c * 2 + (part + 1))
                nc.scalar.activation(part_of(centred, part), part_of(normed, part), ACT.Exp).then_inc(s["is_exp"], 1)

            for step in (square, spread_of, exp_of):
                for part in range(2):
                    step(0, part)

            def chunk(c):
                between = {0: ((square, 0),), 1: ((square, 1),), 2: ((spread_of, 0),), 4: ((spread_of, 1),),
                           6: ((exp_of, 0), (exp_of, 1))}
                for b in range(CHUNK_BLOCKS):
                    act.wait_ge(s["turned"], c * CHUNK_BLOCKS + b + 1)
                    nc.scalar.activation(turned_sb[:, b % 2, :], ps_t[:, b % 2, :], ACT.Copy).then_inc(s["turn_kept"], 1)
                    if not isinstance(c, int):
                        for step, part in between.get(b, ()):
                            step(c + 1, part)
            both(act, chunk)

        @block.tensor
        def _(pe):
            pe.wait_ge(s["w_loaded"], 48)
            for q in range(KQ):
                for r in range(RQ):
                    ins = nc.tensor.transpose((ps_t, ps_h)[q // 2][:, q % 2, r * P:(r + 1) * P], w_rows[:, r, q * P:(q + 1) * P],
                                              k["ident"][:, :])
            ins.then_inc(s["w_turned"], 1)
            for q in range(KQ):
                for r in range(RQ):
                    nc.tensor.matmul(ps_w[:, 0, 2 * q:2 * q + 2], w_rows[:, r, q * P:(q + 1) * P], a_cols[:, r, :],
                                     start=r == 0, stop=r == RQ - 1)
            pe.wait_ge(s["b_widened"], 2)
            for r in range(RQ):
                ins = nc.tensor.matmul(ps_w[:, 1, 0:2], b_wide[:, r, :], a_cols[:, r, :], start=r == 0, stop=r == RQ - 1)
            ins.then_inc(s["wa_made"], 1)
            pe.wait_ge(s["w_kept"], KQ)
            pe.wait_ge(s["wa_kept"], KQ + 1)

            def chunk(c):
                def turn(b):
                    if b in (0, SPLIT):
                        pe.wait_ge(s["is_elu"], c * 2 + (1 if b == 0 else 2))
                    for q in range(KQ):
                        ins = nc.tensor.transpose(ps_t[:, b % 2, q * P:(q + 1) * P],
                                                  elu[:, b * HD + q * P:b * HD + (q + 1) * P], k["ident"][:, :])
                    ins.then_inc(s["turned"], 1)

                turn(0)
                for b in range(CHUNK_BLOCKS):
                    g = c * CHUNK_BLOCKS + b
                    pe.wait_ge(s["turn_kept"], g + 1)
                    if b >= 2:
                        pe.wait_ge(s["rows_made"], g - 1)
                    if b + 1 < CHUNK_BLOCKS:
                        turn(b + 1)
                    for q in range(KQ):
                        ins = nc.tensor.matmul(ps_h[:, b % 2, 0:OUT], turned_sb[:, b % 2, q * P:(q + 1) * P], w_t[:, q, :],
                                               start=q == 0, stop=q == KQ - 1)
                    ins.then_inc(s["products"], 1)
            both(pe, chunk)


def experts(nc, sems, k, sums2, x, g_out, beta_out, router_w, w1_sb, b1, w2_sb, b2, out):
    with ExitStack() as ctx:
        st = Stage(nc, ctx, sems, "moe")
        B = CHUNK_BLOCKS
        KQ = FEAT // P
        TOKENS = B * P
        HALF = TOKENS // 2
        WIDE = B * FEAT
        first = st.sb("first", [P, WIDE])
        work = st.sb("work", [P, WIDE])
        tokens = st.sb("tokens", [P, WIDE])
        result = st.sb("result", [P, WIDE])
        x_raw = st.sb("x_raw", [P, WIDE])
        tokens_t = st.sb("tokens_t", [P, KQ, TOKENS])
        hidden = st.sb("hidden", [P, 2, KQ, TOKENS])
        mean, spread = st.sb("mean", [P, B]), st.sb("spread", [P, B])
        g_row, beta_row = st.sb("g_row", [P, FEAT]), st.sb("beta_row", [P, FEAT])
        b1_col = st.sb("b1_col", [P, EXPERTS, KQ])
        b2_sb = st.sb("b2_sb", [EXPERTS, FEAT])
        router_rows = st.sb("router_rows", [EXPERTS, FEAT])
        router_t = st.sb("router_t", [P, KQ, EXPERTS])
        probs = st.sb("probs", [P, B, EXPERTS])
        top = st.sb("top", [P, B, EXPERTS])
        top_at = st.sb("top_at", [P, B, EXPERTS], U32)
        top_no = st.sb("top_no", [P, B, 2])
        share = st.sb("share", [P, B])
        pick = st.sb("pick", [P, 2, B, EXPERTS])
        combine = st.sb("combine", [P, B, EXPERTS])
        combine_t = st.sb("combine_t", [EXPERTS, TOKENS])
        ps_h = st.ps("ps_h", [P, 4, 512])
        ps_y = st.ps("ps_y", [P, 2, 512])
        ps_t = st.ps("ps_t", [P, 512])
        ps_l = st.ps("ps_l", [P, 512])
        names = ("loaded x_loaded b_loaded vec vec_front is_centred is_squared var_ready std_ready is_normed "
                 "is_affine pool_seq is_negative is_exp turned turn_kept logits reduced is_prob combined combine_turned "
                 "combine_kept router_turned router_kept hidden_made hidden_kept sums_made sums_used finished stored held")
        s = {n: st.sem(n) for n in names.split()}
        VEC, VEC_FRONT = 60, 8
        FRONT = (3, 6, 20, 27, 36, 46, 48, 50, 56, 60)
        SQUARE_1, SPREAD_1, EXP, SQUARE_2, SPREAD_2 = 1, 3, 6, 7, 7
        block = st.block()

        def both(eng, chunk):
            with eng.Fori(0, CHUNKS - 1) as c:
                chunk(c)
            chunk(CHUNKS - 1)

        def by_block(ap):
            return ap.rearrange("p (b f) -> p b f", f=FEAT)

        @block.sync
        def _(sp):
            sp.dma_start(router_rows[:, :], router_w).then_inc(s["loaded"], 16)
            sp.dma_start(g_row[:, :], g_out.partition_broadcast(P)).then_inc(s["loaded"], 16)
            sp.dma_start(beta_row[:, :], beta_out.partition_broadcast(P)).then_inc(s["loaded"], 16)
            sp.dma_start(b2_sb[:, :], b2).then_inc(s["b_loaded"], 16)
            for q in range(KQ):
                sp.dma_start(b1_col[:, :, q], b1[:, q * P:(q + 1) * P].rearrange("e p -> p e"),
                             allow_slow_non_contiguous=True).then_inc(s["b_loaded"], 16)

            with sp.Fori(0, CHUNKS - 1) as c:
                sp.wait_ge(s["finished"], c + 1)
                sp.dma_start(out[bass.ds(c * TOKENS, TOKENS), :].rearrange("(b p) f -> p b f", p=P),
                             by_block(result[:, :])).then_inc(s["stored"], 16)
            c = CHUNKS - 1
            sp.wait_ge(s["finished"], c + 1)
            full = (B - 1) * P
            sp.dma_start(out[c * TOKENS:c * TOKENS + full, :].rearrange("(b p) f -> p b f", p=P),
                         by_block(result[:, :])[:, 0:B - 1, :]).then_inc(s["stored"], 16)
            sp.dma_start(out[c * TOKENS + full:NODES, :], by_block(result[:, :])[0:LAST, B - 1, :]).then_inc(s["stored"], 16)
            sp.wait_ge(s["stored"], 16 * (CHUNKS + 2))

        @block.gpsimd
        def _(pool):
            def load(c, rows_of_last):
                at, full = c * TOKENS, (B - 1) * P
                static = isinstance(c, int)
                most = x[at:at + full, :] if static else x[bass.ds(at, full), :]
                rest = x[at + full:at + full + rows_of_last, :] if static else x[bass.ds(at + full, rows_of_last), :]
                nc.gpsimd.dma_start(by_block(x_raw[:, :])[:, 0:B - 1, :], most.rearrange("(b p) f -> p b f", p=P))\
                    .then_inc(s["x_loaded"], 16)
                nc.gpsimd.dma_start(by_block(x_raw[:, :])[0:rows_of_last, B - 1, :], rest).then_inc(s["x_loaded"], 16)

            load(0, P)
            pool.wait_ge(s["loaded"], 48)

            def affine(c):
                pool.wait_ge(s["is_normed"], c * 2 + 1)
                nc.gpsimd.tensor_tensor(by_block(tokens[:, :]), by_block(tokens[:, :]), middle(g_row[:, :], B), ALU.mult)\
                    .then_inc(s["pool_seq"], 1)
                pool.wait_ge(s["pool_seq"], c + 1)
                nc.gpsimd.tensor_tensor(by_block(tokens[:, :]), by_block(tokens[:, :]), middle(beta_row[:, :], B), ALU.add)\
                    .then_inc(s["is_affine"], 1)

            with pool.Fori(0, CHUNKS - 2) as c:
                affine(c)
                hold(pool, s["is_centred"], c * 2 + 2, s["held"])
                load(c + 1, P)
            affine(CHUNKS - 2)
            pool.wait_ge(s["is_centred"], 2 * (CHUNKS - 1))
            load(CHUNKS - 1, LAST)
            affine(CHUNKS - 1)

        @block.vector
        def _(dve):
            def normalise(seq, raw, c, turn):
                seq.mark(nc.vector.tensor_reduce(mean[:, :], raw, AX.X, ALU.add))
                seq.wait()
                seq.mark(nc.vector.tensor_scalar(mean[:, :], mean[:, :], 1.0 / FEAT, None, ALU.mult))
                yield
                seq.wait()
                nc.vector.tensor_tensor(by_block(work[:, :]), raw, column(mean[:, :], FEAT), ALU.subtract)\
                    .then_inc(s["is_centred"], 1)
                yield
                dve.wait_ge(s["is_squared"], c * 2 + turn)
                nc.vector.tensor_reduce(spread[:, :], by_block(tokens[:, :]), AX.X, ALU.add).then_inc(s["var_ready"], 1)
                yield
                dve.wait_ge(s["std_ready"], c * 2 + turn)
                seq.mark(nc.vector.reciprocal(spread[:, :], spread[:, :]))
                seq.wait()
                nc.vector.tensor_tensor(by_block(tokens[:, :]), by_block(work[:, :]), column(spread[:, :], FEAT), ALU.mult)\
                    .then_inc(s["is_normed"], 1)
                yield

            def front(c):
                seq = Chain(dve, s["vec_front"], c * VEC_FRONT)
                off = c * WIDE
                raw = by_block(sums2[:, off:off + WIDE] if isinstance(c, int) else sums2[:, bass.ds(off, WIDE)])
                yield from normalise(seq, raw, c, 1)
                dve.wait_ge(s["is_affine"], c + 1)
                nc.vector.tensor_scalar(work[:, :], tokens[:, :], 0.0, None, ALU.min).then_inc(s["is_negative"], 1)
                yield
                dve.wait_ge(s["is_exp"], c + 1)
                seq.mark(nc.vector.scalar_tensor_tensor(first[:, :], tokens[:, :], 0.0, work[:, :], ALU.max, ALU.add))
                seq.wait()
                dve.wait_ge(s["x_loaded"], c * 32 + 32)
                seq.mark(nc.vector.scalar_tensor_tensor(first[:, :], first[:, :], -1.0, x_raw[:, :], ALU.add, ALU.add))
                yield
                seq.wait()
                yield from normalise(seq, by_block(first[:, :]), c, 2)
                assert seq.n == VEC_FRONT

            def chunk(c):
                last = isinstance(c, int)
                seq = Chain(dve, s["vec"], c * VEC)
                next_front = None if last else front(c + 1)
                dve.wait_ge(s["logits"], c + 1)
                l3 = ps_l[:, 0:B * EXPERTS].rearrange("p (b e) -> p b e", e=EXPERTS)
                seq.mark(nc.vector.tensor_reduce(share[:, :], l3, AX.X, ALU.max))
                seq.wait()
                nc.vector.tensor_tensor(probs[:, :, :], l3, column(share[:, :], EXPERTS), ALU.subtract).then_inc(s["reduced"], 1)
                dve.wait_ge(s["is_prob"], c + 1)
                seq.mark(nc.vector.tensor_reduce(share[:, :], probs[:, :, :], AX.X, ALU.add))
                seq.wait()
                seq.mark(nc.vector.reciprocal(share[:, :], share[:, :]))
                seq.wait()
                seq.mark(nc.vector.tensor_tensor(probs[:, :, :], probs[:, :, :], column(share[:, :], EXPERTS), ALU.mult))
                hold(dve, s["vec"], seq.base + seq.n, s["held"])
                for b in range(B):
                    seq.mark(nc.vector.max(top[:, b, :], probs[:, b, :]))
                hold(dve, s["vec"], seq.base + seq.n, s["held"])
                for b in range(B):
                    seq.mark(nc.vector.max_index(top_at[:, b, :], top[:, b, :], probs[:, b, :]))
                seq.wait()
                seq.mark(nc.vector.tensor_copy(top_no[:, :, :], top_at[:, :, 0:2]))
                seq.mark(nc.vector.tensor_tensor(share[:, :], top[:, :, 0], top[:, :, 1], ALU.add))
                seq.wait()
                seq.mark(nc.vector.tensor_scalar(share[:, :], share[:, :], 1e-12, None, ALU.max))
                seq.wait()
                seq.mark(nc.vector.reciprocal(share[:, :], share[:, :]))
                for n in range(2):
                    seq.mark(nc.vector.tensor_tensor(pick[:, n, :, :], middle(k["iota"][:, 0:EXPERTS], B),
                                                     column(top_no[:, :, n], EXPERTS), ALU.is_equal))
                seq.wait()
                for n in range(2):
                    seq.mark(nc.vector.tensor_tensor(pick[:, n, :, :], pick[:, n, :, :], column(top[:, :, n], EXPERTS), ALU.mult))
                seq.wait()
                seq.mark(nc.vector.tensor_tensor(combine[:, :, :], pick[:, 0, :, :], pick[:, 1, :, :], ALU.add))
                seq.wait()
                nc.vector.tensor_tensor(combine[:, :, :], combine[:, :, :], column(share[:, :], EXPERTS), ALU.mult)\
                    .then_inc(s["combined"], 1)
                dve.wait_ge(s["stored"], c * 16 + 16)
                seq.mark(nc.vector.tensor_tensor(result[:, :], first[:, :], tokens[:, :], ALU.add))
                seq.wait()
                for e in range(-1, EXPERTS):
                    for b in range(B):
                        n = (e + 1) * B + b
                        dve.wait_ge(s["sums_made"], c * ((EXPERTS + 1) * B) + (n + 1))
                        here = result[:, b * FEAT:(b + 1) * FEAT]
                        if e < 0:
                            ins = nc.vector.tensor_tensor(here, ps_y[:, n % 2, 0:FEAT], here, ALU.add)
                        else:
                            if b == 0:
                                dve.wait_ge(s["sums_used"], c * ((EXPERTS + 1) * B) + n)
                            ins = nc.vector.scalar_tensor_tensor(here, ps_y[:, n % 2, 0:FEAT], combine[:, b, e:e + 1], here,
                                                                 ALU.mult, ALU.add)
                        ins.then_inc(s["sums_used"], 1)
                        if not last and n in FRONT:
                            next(next_front)
                dve.wait_ge(s["sums_used"], (c + 1) * ((EXPERTS + 1) * B))
                dve.sem_inc(s["finished"], 1)
                assert seq.n <= VEC
                dve.sem_inc(s["vec"], VEC - seq.n)
                if not last:
                    assert next(next_front, "all done") == "all done"
            dve.sem_inc(s["stored"], 16)
            for _ in front(0):
                pass
            both(dve, chunk)

        @block.scalar
        def _(act):
            act.wait_ge(s["router_turned"], 1)
            nc.scalar.activation(router_t[:, :, :], ps_t[:, 0:KQ * EXPERTS].rearrange("p (q e) -> p q e", q=KQ), ACT.Copy)\
                .then_inc(s["router_kept"], 1)
            act.wait_ge(s["b_loaded"], 48)

            def square(c, turn):
                act.wait_ge(s["is_centred"], c * 2 + turn)
                nc.scalar.activation(tokens[:, :], work[:, :], ACT.Square).then_inc(s["is_squared"], 1)

            def spread_of(c, turn):
                act.wait_ge(s["var_ready"], c * 2 + turn)
                nc.scalar.activation(spread[:, :], spread[:, :], ACT.Sqrt, bias=k["eps"][:, :], scale=1.0 / FEAT)\
                    .then_inc(s["std_ready"], 1)

            def exp_of(c):
                act.wait_ge(s["is_negative"], c + 1)
                nc.scalar.activation(work[:, :], work[:, :], ACT.Exp).then_inc(s["is_exp"], 1)

            square(0, 1)
            spread_of(0, 1)
            exp_of(0)
            square(0, 2)
            spread_of(0, 2)

            def chunk(c):
                for q in range(KQ * 2):
                    act.wait_ge(s["turned"], c * (KQ * 2) + (q + 1))
                    half, kq = q // KQ, q % KQ
                    span = 4 if half == 0 else B - 4
                    nc.scalar.activation(tokens_t[:, kq, half * 4 * P:(half * 4 + span) * P], ps_h[:, q, 0:span * P], ACT.Copy)\
                        .then_inc(s["turn_kept"], 1)
                act.wait_ge(s["reduced"], c + 1)
                nc.scalar.activation(probs[:, :, :], probs[:, :, :], ACT.Exp).then_inc(s["is_prob"], 1)
                for e in range(EXPERTS):
                    for n in range(4):
                        half, unit = n // 2, n % 2
                        act.wait_ge(s["hidden_made"], c * (4 * EXPERTS) + (4 * e + n + 1))
                        if e >= 2 and n == 0:
                            act.wait_ge(s["sums_made"], c * ((EXPERTS + 1) * B) + e * B)
                        nc.scalar.activation(hidden[:, e % 2, unit, half * HALF:(half + 1) * HALF], ps_h[:, n, 0:HALF], ACT.Gelu,
                                             bias=b1_col[:, e, unit:unit + 1]).then_inc(s["hidden_kept"], 1)
                    if e == 1:
                        act.wait_ge(s["combine_turned"], c * 2 + 1)
                        nc.scalar.activation(combine_t[:, 0:4 * P], ps_t[0:EXPERTS, :], ACT.Copy).then_inc(s["combine_kept"], 1)
                        act.wait_ge(s["combine_turned"], c * 2 + 2)
                        nc.scalar.activation(combine_t[:, 4 * P:TOKENS], ps_t[0:EXPERTS, 0:TOKENS - 4 * P], ACT.Copy)\
                            .then_inc(s["combine_kept"], 1)
                    if not isinstance(c, int):
                        if e == SQUARE_1:
                            square(c + 1, 1)
                        if e == SPREAD_1:
                            spread_of(c + 1, 1)
                        if e == EXP:
                            exp_of(c + 1)
                        if e == SQUARE_2:
                            square(c + 1, 2)
                        if e == SPREAD_2:
                            spread_of(c + 1, 2)
            both(act, chunk)

        @block.tensor
        def _(pe):
            pe.wait_ge(s["loaded"], 48)
            for q in range(KQ):
                ins = nc.tensor.transpose(ps_t[:, q * EXPERTS:(q + 1) * EXPERTS], router_rows[:, q * P:(q + 1) * P],
                                          k["ident"][0:EXPERTS, 0:EXPERTS])
            ins.then_inc(s["router_turned"], 1)
            pe.wait_ge(s["router_kept"], 1)
            pe.wait_ge(s["b_loaded"], 48)

            def chunk(c):
                pe.wait_ge(s["is_normed"], c * 2 + 2)
                for q in range(KQ * 2):
                    half, kq = q // KQ, q % KQ
                    for b in range(4 if half == 0 else B - 4):
                        at = (half * 4 + b) * FEAT + kq * P
                        ins = nc.tensor.transpose(ps_h[:, q, b * P:(b + 1) * P], tokens[:, at:at + P], k["ident"][:, :])
                    ins.then_inc(s["turned"], 1)
                pe.wait_ge(s["turn_kept"], c * (KQ * 2) + KQ * 2)
                for b in range(B):
                    for kq in range(KQ):
                        ins = nc.tensor.matmul(ps_l[:, b * EXPERTS:(b + 1) * EXPERTS], tokens_t[:, kq, b * P:(b + 1) * P],
                                               router_t[:, kq, :], start=kq == 0, stop=kq == KQ - 1)
                ins.then_inc(s["logits"], 1)

                def hidden_of(e):
                    for n in range(4):
                        half, unit = n // 2, n % 2
                        if e:
                            pe.wait_ge(s["hidden_kept"], c * (4 * EXPERTS) + (4 * (e - 1) + n + 1))
                        for kq in range(KQ):
                            ins = nc.tensor.matmul(ps_h[:, n, 0:HALF], w1_sb[:, kq, e, unit * P:(unit + 1) * P],
                                                   tokens_t[:, kq, half * HALF:(half + 1) * HALF],
                                                   start=kq == 0, stop=kq == KQ - 1)
                        ins.then_inc(s["hidden_made"], 1)

                hidden_of(0)
                hidden_of(1)
                pe.wait_ge(s["combined"], c + 1)
                for half in range(2):
                    if half:
                        pe.wait_ge(s["combine_kept"], c * 2 + 1)
                    for b in range(4 if half == 0 else B - 4):
                        ins = nc.tensor.transpose(ps_t[0:EXPERTS, b * P:(b + 1) * P], combine[:, half * 4 + b, :], k["ident"][:, :])
                    ins.then_inc(s["combine_turned"], 1)
                pe.wait_ge(s["combine_kept"], c * 2 + 2)

                def free_bank(n):
                    if n >= 2:
                        pe.wait_ge(s["sums_used"], c * ((EXPERTS + 1) * B) + (n - 1))
                for b in range(B):
                    free_bank(b)
                    nc.tensor.matmul(ps_y[:, b % 2, 0:FEAT], combine_t[:, b * P:(b + 1) * P], b2_sb[:, :], start=True, stop=True)\
                        .then_inc(s["sums_made"], 1)
                for e in range(EXPERTS):
                    if 1 < e + 1 < EXPERTS:
                        hidden_of(e + 1)
                    pe.wait_ge(s["hidden_kept"], c * (4 * EXPERTS) + 4 * (e + 1))
                    for b in range(B):
                        n = (e + 1) * B + b
                        free_bank(n)
                        for unit in range(KQ):
                            ins = nc.tensor.matmul(ps_y[:, n % 2, 0:FEAT], hidden[:, e % 2, unit, b * P:(b + 1) * P],
                                                   w2_sb[:, unit, e, :], start=unit == 0, stop=unit == KQ - 1)
                        ins.then_inc(s["sums_made"], 1)
            both(pe, chunk)


def build(nc, t):
    with ExitStack() as ctx, ExitStack() as sems:
        k = constants(nc, ctx, sems)
        shared = Stage(nc, ctx, sems, "shared")
        s_src1 = shared.sb("s_src1", [P, BLOCKS, HEADS])
        node_of = shared.sb("node_of", [P, STEPS], I32)
        local_of = shared.sb("local_of", [P, STEPS])
        step_info = shared.sb("step_info", [P, STEPS * 2], I32)
        s_src2 = shared.sb("s_src2", [P, BLOCKS])
        table1 = nc.dram_tensor("table1", [NODES, ROW1], FP32, kind="Internal").ap()
        table2 = nc.dram_tensor("table2", [NODES, ROW2], FP32, kind="Internal").ap()
        gnn = {n: t["L0_gnn_" + n] for n in ("W_heads b_heads a_heads g_heads beta_heads W_out b_out a_out g_out beta_out").split()}
        ffn = {n: t["L0_ffn_" + n] for n in "router_w w1 b1 w2 b2".split()}

        project_heads(nc, sems, k, t["x"], gnn["W_heads"], gnn["b_heads"], gnn["a_heads"], table1, s_src1)
        sort_edges(nc, sems, k, t["src"], t["dst"], node_of, local_of, step_info)
        with ExitStack() as heads:
            sums1 = heads.enter_context(nc.sbuf_tensor("sums1", [P, (BLOCKS + NOWHERES) * HD], FP32))
            aggregate(nc, sems, k, "heads", table1, ROW1, HD, HEADS, s_src1[:, :, :].rearrange("p b h -> p (b h)"),
                      node_of, local_of, step_info, sums1)
            project_out(nc, sems, k, sums1, gnn["g_heads"], gnn["beta_heads"], gnn["W_out"], gnn["b_out"], gnn["a_out"],
                        table2, s_src2)
        late = Stage(nc, ctx, sems, "late")
        sums2 = late.sb("sums2", [P, (BLOCKS + NOWHERES) * FEAT])
        w1_sb = late.sb("w1", [P, FEAT // P, EXPERTS, FEAT])
        w2_sb = late.sb("w2", [P, FEAT // P, EXPERTS, FEAT])
        loads = [(sb[:, q, :, :], w[:, q * P:(q + 1) * P, :].rearrange("e p f -> p e f"))
                 for sb, w in ((w1_sb, ffn["w1"]), (w2_sb, ffn["w2"])) for q in range(FEAT // P)]
        aggregate(nc, sems, k, "out", table2, ROW2, FEAT, 1, s_src2, node_of, local_of, step_info, sums2, loads)
        experts(nc, sems, k, sums2, t["x"], gnn["g_out"], gnn["beta_out"], ffn["router_w"], w1_sb, ffn["b1"], w2_sb,
                ffn["b2"], t["out"])


def kernel(**inputs):
    import numpy as np
    import concourse.bacc as bacc
    from concourse.bass_utils import run_bass_kernel_spmd as run

    nc = bacc.Bacc("TRN2", target_bir_lowering=False, num_devices=1)
    arrays, tensors = {}, {}
    for name, value in inputs.items():
        arrays[f"in_{name}"] = a = np.ascontiguousarray(value)
        tensors[name] = nc.dram_tensor(f"in_{name}", a.shape, mybir.dt.from_np(a.dtype), kind="ExternalInput").ap()
    tensors["out"] = nc.dram_tensor("out", (NODES, FEAT), FP32, kind="ExternalOutput").ap()
    build(nc, tensors)
    return run(nc, [arrays], core_ids=[0]).results[0]["out"]
```
